# Optimizing a Trainium2 kernel written in Bass

```python
import numpy as np
import jax
import jax.numpy as jnp

def _softmax(x, axis=-1):
    return jax.nn.softmax(x, axis=axis)
def _gelu(x):
    return jax.nn.gelu(x, approximate=True)
def _silu(x):
    return jax.nn.silu(x)
def _sigmoid(x):
    return jax.nn.sigmoid(x)
def _layernorm(x, axis=-1, eps=1e-5):
    m = jnp.mean(x, axis=axis, keepdims=True)
    v = jnp.var(x, axis=axis, keepdims=True)
    return (x - m) / jnp.sqrt(v + eps)
def _scatter_add(tgt, idx, src, axis=0):
    return tgt.at[idx].add(src)
def _segment_sum(src, seg, n):
    return jax.ops.segment_sum(src, seg, n)

kernel_name = 'mk_adj_preln_d2_adj_64_abb032'

def setup_inputs(seed: int = 0):
    np.random.seed(seed)
    _w = jnp.asarray
    def _rec_inputs():
        import jax
        import jax.numpy as jnp
        _gk = jax.random.key(seed)
        x = -0.006082 + 1.001 * jax.random.normal(jax.random.fold_in(_gk, 1), (8192, 64), jnp.float32)
        _a = jax.random.bernoulli(jax.random.fold_in(_gk, 2), 0.000976562, (8192, 8192))
        _a = jnp.logical_or(_a, jnp.swapaxes(_a, -1, -2))
        _a = jnp.logical_or(_a, jnp.eye(8192, dtype=bool))
        adj = _a.astype(jnp.int32)
        return x, adj
    x, adj = _rec_inputs()
    def _L0_gnn_setup():
        import jax, jax.numpy as jnp
        import numpy as np
        ALPHA = 0.2
        NEG_INF = -9000000000000000.0
        key = jax.random.key(seed)
        k1, k2, k3, k4 = jax.random.split(key, 4)
        N, F_IN, F_OUT = (1024, 64, 64)
        h = jax.random.normal(k1, (N, F_IN), dtype=jnp.float32)
        adj = jax.random.randint(k2, (N, N), 0, 2, dtype=jnp.int32)
        lim_W = 1.414 * np.sqrt(6.0 / (F_IN + F_OUT))
        W = jax.random.uniform(k3, (F_IN, F_OUT), minval=-lim_W, maxval=lim_W, dtype=jnp.float32)
        lim_a = 1.414 * np.sqrt(6.0 / (2 * F_OUT + 1))
        a = jax.random.uniform(k4, (2 * F_OUT, 1), minval=-lim_a, maxval=lim_a, dtype=jnp.float32)
        return {'h': h, 'adj': adj, 'W': W, 'a': a}
    _L0_gnn_all = _L0_gnn_setup()
    _L0_gnn_in = {k: v for k, v in _L0_gnn_all.items() if k in ('W', 'a', )}
    del _L0_gnn_all

    def _L1_gnn_setup():
        import jax, jax.numpy as jnp
        import numpy as np
        N = 8192
        F_IN = 64
        F_OUT = 64
        ALPHA = 0.2
        NEG_INF = -9000000000000000.0
        key = jax.random.key(seed)
        k1, k2, k3, k4 = jax.random.split(key, 4)
        h = jax.random.normal(k1, (N, F_IN), dtype=jnp.float32)
        adj = jax.random.randint(k2, (N, N), 0, 2, dtype=jnp.int32)
        W = jax.random.normal(k3, (F_OUT, F_IN), dtype=jnp.float32) * (1.0 / np.sqrt(F_IN))
        a = jax.random.normal(k4, (2 * F_OUT,), dtype=jnp.float32) * (1.0 / np.sqrt(2 * F_OUT))
        return {'h': h, 'adj': adj, 'W': W, 'a': a}
    _L1_gnn_all = _L1_gnn_setup()
    _L1_gnn_in = {k: v for k, v in _L1_gnn_all.items() if k in ('W', 'a', )}
    del _L1_gnn_all

    return {
        "x": x,
        "adj": adj,
        "L0_gnn_W": _L0_gnn_in["W"],
        "L0_gnn_a": _L0_gnn_in["a"],
        "L1_gnn_W": _L1_gnn_in["W"],
        "L1_gnn_a": _L1_gnn_in["a"],
    }

def reference(x, adj, L0_gnn_W, L0_gnn_a, L1_gnn_W, L1_gnn_a):
    import jax
    import jax.numpy as jnp
    def _L0_gnn_ref(h, adj, W, a):
        import jax, jax.numpy as jnp
        import numpy as np
        ALPHA = 0.2
        NEG_INF = -9000000000000000.0
        F_OUT = W.shape[1]
        Wh = h @ W
        a1, a2 = (a[:F_OUT, 0], a[F_OUT:, 0])
        e = (Wh @ a1)[:, None] + (Wh @ a2)[None, :]
        e = jax.nn.leaky_relu(e, negative_slope=ALPHA)
        scores = jnp.where(adj > 0, e, jnp.float32(NEG_INF))
        attention = jax.nn.softmax(scores, axis=1)
        h_prime = attention @ Wh
        return jax.nn.elu(h_prime)

    def _L1_gnn_ref(h, adj, W, a):
        import jax, jax.numpy as jnp
        import numpy as np
        N = 8192
        F_IN = 64
        F_OUT = 64
        ALPHA = 0.2
        NEG_INF = -9000000000000000.0
        Wh = h @ W.T
        a1, a2 = (a[:F_OUT], a[F_OUT:])
        src = Wh @ a1
        dst = Wh @ a2
        e = jax.nn.leaky_relu(src[:, None] + dst[None, :], negative_slope=ALPHA)
        scores = jnp.where(adj > 0, e, NEG_INF)
        attention = jax.nn.softmax(scores, axis=1)
        h_prime = attention @ Wh
        return jax.nn.elu(h_prime)

    h = jnp.maximum(_layernorm(x, axis=-1), 0.0)
    x = x + _L0_gnn_ref(h, adj, L0_gnn_W, L0_gnn_a)
    h = jnp.maximum(_layernorm(x, axis=-1), 0.0)
    x = x + _L1_gnn_ref(h, adj, L1_gnn_W, L1_gnn_a)
    return x


_drawn_inputs = setup_inputs


def setup_inputs(seed=0):
    import zlib

    import numpy as np

    out = dict(_drawn_inputs(seed))
    spreads = {}
    factors = {}
    for name, (base, spread) in spreads.items():
        noise = np.random.default_rng([zlib.crc32(name.encode()), seed]).standard_normal(out[name].shape)
        drawn = base * np.exp(spread * noise) if base else spread * noise
        out[name] = jnp.asarray(drawn.astype(out[name].dtype))
    for name, factor in factors.items():
        out[name] = (out[name] * factor).astype(out[name].dtype)
    return out
```

```python
from contextlib import ExitStack

import numpy as np
import concourse.bass as bass
from concourse import mybir

ALU = mybir.AluOpType
ACT = mybir.ActivationFunctionType
AX = mybir.AxisListType
F32 = mybir.dt.float32
BF16 = mybir.dt.bfloat16
I32 = mybir.dt.int32
U16 = mybir.dt.uint16

P = 128
LEAK = 0.2
EPS = 1e-5
BITS = 16
MARK = 0x4000
STEEP = 1e20


def gat2_kernel(nc, x, adj, w0, a0, w1, a1, out):
    N, F = x.shape
    TILES = N // P
    GT = 4
    GROUP = GT * P
    GROUPS = N // GROUP
    CT = 4
    CHUNKS = TILES // CT
    UT = 16
    UNPACKS = TILES // UT
    CPU = UT // CT
    WPT = P // BITS
    LW = 1024
    LT = LW // P
    STEPS = N // LW
    GSTEPS = GT * STEPS
    PACE = 3
    WLAG = 2 if STEPS >= 8 else 1
    H = F + 1
    W3 = 3 * H
    QT = TILES // 4
    QB = QT // GT
    SB = 8
    SPLITS = TILES // SB
    TOG = 4
    assert UNPACKS % 2 == 0 and CHUNKS % TOG == 0

    def steps_at(c):
        return [s for s in range(GSTEPS) if s // PACE == c]

    def words_at(c):
        return [k for k in range(GT) if min((k * STEPS + STEPS - 1) // PACE + WLAG, CHUNKS - 1) == c]

    with ExitStack() as ctx:
        def sb(name, shape, dt):
            return ctx.enter_context(nc.sbuf_tensor(name, shape, dt))

        def sem(name):
            return ctx.enter_context(nc.semaphore(name))

        x1 = nc.dram_tensor("x1_scratch", (N, F), F32)
        s_dram = nc.dram_tensor("s_scratch", (2, N), F32)
        psum = ctx.enter_context(nc.psum_tensor("psum", [P, 8, 512], F32))

        words = sb("words", [P, TILES, N // BITS], U16)
        parts = sb("parts", [P, TILES, 2, 3, H], BF16)
        work = sb("work", [P, 2 * UT * GROUP], U16)
        toggle = sb("toggle", [P, TOG * CT * GROUP], U16)
        stage = sb("stage", [P, 4, LW], I32)
        natural = sb("natural", [P, 2, LW], BF16)
        s_row = sb("s_row", [P, 2, GROUP], F32)
        sums = sb("sums", [P, GT, 6, H], F32)
        sum3 = sb("sum3", [P, GT, 3, H], F32)
        x_tile = sb("x_tile", [P, GT, F], F32)
        y_tile = sb("y_tile", [P, GT, F], F32)
        hneg = sb("hneg", [P, GT, F], F32)
        th = sb("th", [P, GT, F], F32)
        tmp = sb("tmp", [P, GT, F], F32)
        flag = sb("flag", [P, GT, 1], F32)
        den = sb("den", [P, GT, 1], F32)
        rden = sb("rden", [P, GT, 1], F32)
        ident = sb("ident", [P, P], F32)
        pack_w = sb("pack_w", [P, WPT], BF16)
        zero_w = sb("zero_w", [P, P], BF16)
        wrow = sb("wrow", [F, 2, F], F32)
        wcol = sb("wcol", [F, 2, F], F32)
        acol = sb("acol", [F, 2, 2], F32)
        waug = sb("waug", [F, 2, F + 2], F32)
        ones = sb("ones", [P, P], F32)
        mean = sb("mean", [P, TILES], F32)
        var = sb("var", [P, TILES], F32)
        std = sb("std", [P, TILES], F32)
        rstd = sb("rstd", [P, TILES], F32)
        newton = sb("newton", [P, TILES], F32)
        sd = sb("sd", [P, TILES, 2], F32)
        dg = sb("dg", [P, 2, TILES], F32)
        uv = sb("uv", [P, 2, TILES], F32)
        steep_d = sb("steep_d", [P, TILES], F32)
        zc = sb("zc", [P, 4, TILES], F32)
        cmax = sb("cmax", [P, 4], F32)
        whsum = sb("whsum", [P, F], F32)
        whmean = sb("whmean", [P, F], F32)
        half_steep = sb("half_steep", [P, 1], F32)

        bits = work.rearrange("p (s j i) -> p s j i", s=2, j=UT)
        tog = toggle.rearrange("p (s j i) -> p s j i", s=TOG, j=CT)
        xall = toggle[:, 0:2 * TILES * F].bitcast(F32).rearrange("p (t f) -> p t f", t=TILES)
        work_f = work[:, :].bitcast(F32)
        wh = work_f[:, 0:TILES * H].rearrange("p (t h) -> p t h", t=TILES)
        o = TILES * H
        rest = work_f[:, o:o + 4 * SB * H].rearrange("p (b s t h) -> p b s t h", b=2, s=2, t=SB)
        o += 4 * SB * H
        ht = work_f[0:F, o:o + 2 * GROUP].rearrange("p (s i) -> p s i", s=2)
        square = work_f[:, 0:QT * F].rearrange("p (t f) -> p t f", t=QT)
        srow_sb = sums[0:1, :, :, :].rearrange("p a b c -> p (a b c)")[:, 0:2 * GROUP].rearrange(
            "p (s i) -> p s i", s=2)
        hot = sums[:, :, :, :].rearrange("p a b c -> p (a b c)")[:, 0:P]
        power = sums[:, :, :, :].rearrange("p a b c -> p (a b c)")[:, P:2 * P]

        const_in = sem("const_in")
        const_pool = sem("const_pool")
        const_dve = sem("const_dve")
        apart = sem("apart")
        const_pe = sem("const_pe")
        x_in = [sem(f"x_in{q}") for q in range(4)]
        chain = sem("chain")
        var_ready = sem("var_ready")
        std_ready = sem("std_ready")
        h_ready = sem("h_ready")
        turned = sem("turned")
        ht_ready = sem("ht_ready")
        s_mm = sem("s_mm")
        wh_mm = sem("wh_mm")
        wh_free = sem("wh_free")
        srow_free = sem("srow_free")
        s_stored = [sem("s_stored0"), sem("s_stored1")]
        dmax_part = sem("dmax_part")
        dmax_ready = sem("dmax_ready")
        exp_in = sem("exp_in")
        exp_ready = sem("exp_ready")
        whsum_ready = sem("whsum_ready")
        whmean_mm = sem("whmean_mm")
        whmean_ready = sem("whmean_ready")
        scaled = [sem("scaled_dve"), sem("scaled_pool")]
        hi_ready = [sem("hi_dve"), sem("hi_pool")]
        rest1 = [sem("rest1_dve"), sem("rest1_pool")]
        mid_ready = [sem("mid_dve"), sem("mid_pool")]
        parts_ready = [sem("parts_dve"), sem("parts_pool")]
        stage_in = [sem(f"stage_in{s}") for s in range(4)]
        conv = [sem("conv_act"), sem("conv_dve")]
        packed = sem("packed")
        stored = sem("stored")
        row_in = sem("row_in")
        sign_ready = sem("sign_ready")
        chunk_used = sem("chunk_used")
        unpacked = sem("unpacked")
        anded = sem("anded")
        masks_ready = sem("masks_ready")
        bank_done = sem("bank_done")
        bank_free = sem("bank_free")
        sums_free = sem("sums_free")
        neg_ready = sem("neg_ready")
        tanh_ready = sem("tanh_ready")
        den_ready = sem("den_ready")
        den_inv = sem("den_inv")
        half_ready = sem("half_ready")
        half_inv = sem("half_inv")
        pool_step = sem("pool_step")
        xt_in = sem("xt_in")
        y_stored = sem("y_stored")

        def settled(eng):
            eng.sem_inc(apart, 1)

        adj_t = adj.rearrange("(r p) (l w) -> r p l w", p=P, w=LW)
        block = ctx.enter_context(nc.Block())
        src_of = [x, x1[:, :]]
        dst_of = [x1[:, :], out]

        @block.sync
        def _(sp):
            sp.dma_start(wrow[:, 0, :], w0).then_inc(const_in, 16)
            sp.dma_start(wrow[:, 1, :], w1).then_inc(const_in, 16)
            for k in range(2):
                sp.dma_start(acol[:, 0, k:k + 1], a0[k * F:(k + 1) * F, :]).then_inc(const_in, 16)
                sp.dma_start(acol[:, 1, k:k + 1], a1[k * F:(k + 1) * F].unsqueeze(1)).then_inc(const_in, 16)

            def load_x(L):
                src = src_of[L].rearrange("(t p) f -> p t f", p=P)
                for q in range(4):
                    sp.dma_start(xall[:, q * QT:(q + 1) * QT, :], src[:, q * QT:(q + 1) * QT, :]).then_inc(x_in[q], 16)

            def store_s(L):
                with sp.Fori(0, GROUPS // 2) as i:
                    for par in range(2):
                        b = i * 2 + par
                        sp.wait_ge(srow_free, b + (L * GROUPS + 3))
                        sp.dma_start(s_dram[L:L + 1, bass.ds(b * GROUP, GROUP)],
                                     srow_sb[:, par, :]).then_inc(s_stored[par], 16)

            def load_adj(row_tile, first_step, steps=range(STEPS)):
                for s in steps:
                    slot = s % 4
                    sp.wait_ge(conv[s % 2], (first_step + s - s % 2) // 2 + 1)
                    sp.dma_start(stage[:, slot, :], adj_t[bass.ds(row_tile, 1), :, s, :].rearrange("r p w -> (r p) w")
                                 ).then_inc(stage_in[slot], 16)

            def load_row(L, g):
                gg = g + L * GROUPS
                if not (isinstance(g, int) and g + L == 0):
                    sp.wait_ge(row_in, gg * 16)
                sp.dma_start(s_row[:, g % 2, :] if isinstance(g, int) else s_row[:, bass.ds(g % 2, 1), :].rearrange("p o i -> p (o i)"),
                             s_dram[L:L + 1, bass.ds(g * GROUP, GROUP)].to_broadcast((P, GROUP))).then_inc(row_in, 16)

            load_x(0)
            load_adj(0, 0, range(4))
            store_s(0)
            load_adj(0, 0, range(4, STEPS))
            with sp.Fori(1, GT) as r:
                load_adj(r, r * STEPS)
            for par in range(2):
                sp.wait_ge(s_stored[par], 16 * (GROUPS // 2 + 1))
            load_row(0, 0)
            load_row(0, 1)
            with sp.Fori(1, GROUPS - 1) as g:
                for k in range(GT):
                    load_adj(g * GT + k, (g * GT + k) * STEPS)
                sp.wait_ge(sign_ready, g * CHUNKS)
                load_row(0, g + 1)
            for k in range(GT):
                load_adj((GROUPS - 1) * GT + k, ((GROUPS - 1) * GT + k) * STEPS)

            sp.wait_ge(y_stored, 16 * GROUPS)
            sp.wait_ge(chunk_used, TOG + GROUPS * CHUNKS)
            load_x(1)
            store_s(1)
            for par in range(2):
                sp.wait_ge(s_stored[par], 16 * (GROUPS + 1))
            load_row(1, 0)
            load_row(1, 1)
            with sp.Fori(2, GROUPS) as g:
                sp.wait_ge(sign_ready, (g + GROUPS - 1) * CHUNKS)
                load_row(1, g)

        @block.scalar
        def _(act):
            act.sem_inc(conv[0], 2)
            act.sem_inc(srow_free, 2)
            act.sem_inc(bank_free, GT)
            for par in range(2):
                act.sem_inc(s_stored[par], 16)

            def prepare(L):
                act.wait_ge(var_ready, L + 1)
                nc.scalar.activation(std[:, :], var[:, :], ACT.Sqrt).then_inc(std_ready, 1)
                with act.Fori(0, 4) as q:
                    for k in range(QB):
                        b = q * QB + (L * GROUPS + k)
                        act.wait_ge(turned, b + 1)
                        nc.scalar.activation(ht[:, k % 2, :], psum[0:F, k % 2, :], ACT.Relu).then_inc(ht_ready, 1)
                        act.wait_ge(s_mm, b + 1)
                        act.wait_ge(s_stored[k % 2], (q * (QB // 2) + ((L * GROUPS + k) // 2 + 1)) * 16)
                        nc.scalar.copy(srow_sb[:, k % 2, :], psum[0:1, 6 + k % 2, :]).then_inc(srow_free, 1)
                act.wait_ge(exp_in, L + 1)
                nc.scalar.activation(dg[:, 0, :], sd[:, :, 1], ACT.Exp, bias=cmax[:, 1:2])
                nc.scalar.activation(dg[:, 1, :], sd[:, :, 1], ACT.Exp, bias=cmax[:, 2:3], scale=LEAK)
                nc.scalar.activation(uv[:, 0, :], zc[:, 2, :], ACT.Exp)
                nc.scalar.activation(uv[:, 1, :], zc[:, 3, :], ACT.Exp).then_inc(exp_ready, 1)
                with act.Fori(0, SPLITS // 2) as i:
                    for part, have, done in ((0, scaled, hi_ready), (1, rest1, mid_ready)):
                        for k in range(2):
                            for e in range(2):
                                act.wait_ge(have[e], i * 2 + (L * SPLITS + k + 1))
                                settled(act)
                                nc.scalar.copy(parts[:, bass.ds((i * 2 + k) * SB, SB), e, part, :],
                                               rest[:, e, k, :, :]).then_inc(done[e], 1)
                act.wait_ge(whmean_mm, L + 1)
                nc.scalar.mul(whmean[:, :], psum[:, 7, 0:F], 1.0 / N).then_inc(whmean_ready, 1)

            def convert(g, s):
                step = g * GSTEPS + s
                act.wait_ge(stage_in[s % 4], (g * (GSTEPS // 4) + (s // 4 + 1)) * 16)
                act.wait_ge(packed, step + 1)
                nc.scalar.activation(natural[:, 0, :], stage[:, s % 4, :], ACT.Sigmoid,
                                     scale=200.0, bias=half_steep[:, 0:1]).then_inc(conv[0], 1)

            def signs(L, g, c):
                n = (g + L * GROUPS) * CHUNKS + c
                act.wait_ge(chunk_used, n + 1)
                slot = g % 2
                row = s_row[:, slot, :] if isinstance(g, int) else s_row[:, bass.ds(slot, 1), :].rearrange("p o i -> p (o i)")
                settled(act)
                for j in range(CT):
                    t = c * CT + j
                    ins = nc.scalar.activation(tog[:, c % TOG, j, :].bitcast(BF16), row, ACT.Relu,
                                               scale=STEEP, bias=steep_d[:, t:t + 1])
                ins.then_inc(sign_ready, 1)

            def take_sums(L, g):
                gg = g + L * GROUPS
                act.wait_ge(sums_free, gg + 1)
                for r in range(GT):
                    act.wait_ge(bank_done, gg * GT + r + 1)
                    settled(act)
                    for e in range(2):
                        ins = nc.scalar.activation(sums[:, r, 3 * e:3 * e + 3, :].rearrange("p k h -> p (k h)"),
                                                   psum[:, r, e * W3:(e + 1) * W3], ACT.Copy,
                                                   scale=uv[:, e, bass.ds(g * GT + r, 1)])
                    ins.then_inc(bank_free, 1)

            def tanh(L, g):
                gg = g + L * GROUPS
                act.wait_ge(neg_ready, gg + 1)
                nc.scalar.activation(th[:, :, :], hneg[:, :, :], ACT.Tanh, scale=0.5).then_inc(tanh_ready, 1)

            def group(L, g, packing, first):
                if L == 0 or True:
                    act.wait_ge(row_in, (g + L * GROUPS + 1) * 16)
                for c in range(CHUNKS):
                    if packing:
                        for s in steps_at(c):
                            if s % 2 == 0:
                                convert(g + 1, s)
                    signs(L, g, c)
                    if not first:
                        if c == 1:
                            take_sums(L, g - 1)
                        if c == 5:
                            tanh(L, g - 1)

            act.wait_ge(const_dve, 2)
            prepare(0)
            for s in range(0, GSTEPS, 2):
                convert(0, s)
            group(0, 0, True, True)
            with act.Fori(1, GROUPS - 1) as g:
                group(0, g, True, False)
            group(0, GROUPS - 1, False, False)
            take_sums(0, GROUPS - 1)
            tanh(0, GROUPS - 1)
            prepare(1)
            group(1, 0, False, True)
            with act.Fori(1, GROUPS) as g:
                group(1, g, False, False)
            take_sums(1, GROUPS - 1)
            tanh(1, GROUPS - 1)

        @block.gpsimd
        def _(pool):
            pool.sem_inc(sums_free, 1)
            pool.sem_inc(parts_ready[1], 2)
            nc.gpsimd.memset(ident[:, :], 0.0).then_inc(const_pool, 1)
            pool.wait_ge(const_pool, 1)
            nc.gpsimd.affine_select(out=ident[:, :], in_=ident[:, :], compare_op=ALU.not_equal, fill=1.0, base=0,
                                    pattern=[[-1, P]], channel_multiplier=1).then_inc(const_pool, 1)

            def split(L):
                pool.wait_ge(exp_ready, L + 1)
                with pool.Fori(0, SPLITS // 2) as i:
                    for k in range(2):
                        t = bass.ds((i * 2 + k) * SB, SB)
                        pool.wait_ge(parts_ready[1], i * 2 + (L * SPLITS + 2))
                        settled(pool)
                        nc.gpsimd.tensor_tensor(rest[:, 1, k, :, :], wh[:, t, :],
                                                dg[:, 1, t].unsqueeze(2).to_broadcast((P, SB, H)),
                                                ALU.mult).then_inc(scaled[1], 1)
                    for k in range(2):
                        t = bass.ds((i * 2 + k) * SB, SB)
                        pool.wait_ge(hi_ready[1], i * 2 + (L * SPLITS + k + 1))
                        nc.gpsimd.tensor_tensor(rest[:, 1, k, :, :], rest[:, 1, k, :, :], parts[:, t, 1, 0, :],
                                                ALU.subtract).then_inc(rest1[1], 1)
                    for k in range(2):
                        t = bass.ds((i * 2 + k) * SB, SB)
                        pool.wait_ge(mid_ready[1], i * 2 + (L * SPLITS + k + 1))
                        nc.gpsimd.tensor_tensor(parts[:, t, 1, 2, :], rest[:, 1, k, :, :], parts[:, t, 1, 1, :],
                                                ALU.subtract).then_inc(parts_ready[1], 1)

            STEP = 10

            def finish(L, g):
                gg = g + L * GROUPS
                done = [0]

                def link(ins):
                    done[0] += 1
                    ins.then_inc(pool_step, 1)
                    pool.wait_ge(pool_step, gg * STEP + done[0])
                    settled(pool)

                src = src_of[L].rearrange("(t p) f -> p t f", p=P)
                dst = dst_of[L].rearrange("(t p) f -> p t f", p=P)
                settled(pool)
                pool.dma_start(x_tile[:, :, :], src[:, bass.ds(g * GT, GT), :]).then_inc(xt_in, 16)
                pool.wait_ge(bank_free, (gg + 1) * GT + GT)
                link(nc.gpsimd.tensor_tensor(sum3[:, :, :, :], sums[:, :, 0:3, :], sums[:, :, 3:6, :], ALU.add))
                pool.sem_inc(sums_free, 1)
                link(nc.gpsimd.tensor_tensor(sum3[:, :, 1, :], sum3[:, :, 1, :], sum3[:, :, 2, :], ALU.add))
                link(nc.gpsimd.tensor_tensor(sum3[:, :, 0, :], sum3[:, :, 0, :], sum3[:, :, 1, :], ALU.add))
                link(nc.gpsimd.tensor_scalar(flag[:, :, :], sum3[:, :, 0, F:H], 0.0, None, ALU.is_equal))
                nc.gpsimd.tensor_tensor(den[:, :, :], sum3[:, :, 0, F:H], flag[:, :, :], ALU.add).then_inc(den_ready, 1)
                link(nc.gpsimd.tensor_tensor(tmp[:, :, :], flag[:, :, :].to_broadcast((P, GT, F)),
                                             whmean[:, :].unsqueeze(1).to_broadcast((P, GT, F)), ALU.mult))
                link(nc.gpsimd.tensor_tensor(tmp[:, :, :], tmp[:, :, :], sum3[:, :, 0, 0:F], ALU.add))
                pool.wait_ge(den_inv, gg + 1)
                settled(pool)
                link(nc.gpsimd.tensor_tensor(tmp[:, :, :], tmp[:, :, :],
                                             rden[:, :, :].to_broadcast((P, GT, F)), ALU.mult))
                nc.gpsimd.tensor_scalar(hneg[:, :, :], tmp[:, :, :], 0.0, None, ALU.min).then_inc(neg_ready, 1)
                pool.wait_ge(tanh_ready, gg + 1)
                settled(pool)
                nc.gpsimd.tensor_scalar(hneg[:, :, :], th[:, :, :], -0.5, 0.5, ALU.mult, ALU.add).then_inc(half_ready, 1)
                pool.wait_ge(half_inv, gg + 1)
                link(nc.gpsimd.tensor_tensor(hneg[:, :, :], th[:, :, :], hneg[:, :, :], ALU.mult))
                nc.gpsimd.tensor_scalar(tmp[:, :, :], tmp[:, :, :], 0.0, None, ALU.max)
                pool.wait_ge(xt_in, (gg + 1) * 16)
                link(nc.gpsimd.tensor_tensor(hneg[:, :, :], hneg[:, :, :], x_tile[:, :, :], ALU.add))
                link(nc.gpsimd.tensor_tensor(y_tile[:, :, :], hneg[:, :, :], tmp[:, :, :], ALU.add))
                assert done[0] == STEP, done[0]
                pool.dma_start(dst[:, bass.ds(g * GT, GT), :], y_tile[:, :, :]).then_inc(y_stored, 16)
                pool.wait_ge(y_stored, (gg + 1) * 16)

            for L in range(2):
                pool.wait_ge(dmax_part, L + 1)
                nc.gpsimd.partition_all_reduce(cmax[:, 0:1], cmax[:, 3:4], P,
                                               bass.bass_isa.ReduceOp.max).then_inc(dmax_ready, 1)
                split(L)
                pool.wait_ge(whmean_ready, L + 1)
                with pool.Fori(0, GROUPS) as g:
                    finish(L, g)

        @block.vector
        def _(dve):
            dve.sem_inc(conv[1], 2)
            dve.sem_inc(wh_free, 2)
            dve.sem_inc(stored, 2)
            dve.sem_inc(parts_ready[0], 2)
            links = [0]

            def link(ins):
                links[0] += 1
                ins.then_inc(chain, 1)
                dve.wait_ge(chain, links[0])

            def constants():
                nc.vector.memset(ones[:, :], 1.0)
                nc.vector.memset(half_steep[:, :], -100.0)
                nc.vector.memset(zero_w[:, :], 0.0).then_inc(const_dve, 1)
                for t in range(BITS):
                    ins = nc.vector.memset(power[:, t * WPT:(t + 1) * WPT], float(2 ** t))
                link(ins)
                dve.wait_ge(const_pool, 2)
                link(nc.vector.tensor_tensor(hot, ident[:, :], power, ALU.mult))
                link(nc.vector.tensor_reduce(power[:, 0:WPT], hot.rearrange("p (t m) -> p m t", t=BITS), AX.X, ALU.add))
                nc.vector.tensor_copy(pack_w[:, :], power[:, 0:WPT]).then_inc(const_dve, 1)
                dve.wait_ge(const_pe, 1)
                nc.vector.tensor_copy(wcol[:, :, :], psum[0:F, 0, 0:2 * F].rearrange("p (l f) -> p l f", l=2)
                                      ).then_inc(const_dve, 1)
                dve.wait_ge(const_pe, 2)
                nc.vector.tensor_copy(waug[:, :, F:F + 2], psum[0:F, 1, 0:4].rearrange("p (l k) -> p l k", l=2))
                nc.vector.tensor_copy(waug[:, 0, 0:F], wrow[:, 0, :])
                nc.vector.tensor_copy(waug[:, 1, 0:F], wcol[:, 1, :]).then_inc(const_dve, 1)

            def prepare(L):
                for q in range(4):
                    t = slice(q * QT, (q + 1) * QT)
                    dve.wait_ge(x_in[q], 16 * (L + 1))
                    link(nc.vector.tensor_reduce(mean[:, t], xall[:, t, :], AX.X, ALU.add))
                    link(nc.vector.tensor_scalar(mean[:, t], mean[:, t], -1.0 / F, None, ALU.mult))
                    link(nc.vector.tensor_tensor(xall[:, t, :], xall[:, t, :],
                                                 mean[:, t].unsqueeze(2).to_broadcast((P, QT, F)), ALU.add))
                    link(nc.vector.tensor_tensor(square[:, :, :], xall[:, t, :], xall[:, t, :], ALU.mult))
                    link(nc.vector.tensor_reduce(var[:, t], square[:, :, :], AX.X, ALU.add))
                link(nc.vector.tensor_scalar(var[:, :], var[:, :], 1.0 / F, EPS, ALU.mult, ALU.add))
                dve.sem_inc(var_ready, 1)
                nc.vector.memset(wh[:, :, F:H], 1.0)
                dve.wait_ge(std_ready, L + 1)
                link(nc.vector.reciprocal(rstd[:, :], std[:, :]))
                link(nc.vector.tensor_tensor(newton[:, :], rstd[:, :], rstd[:, :], ALU.mult))
                link(nc.vector.tensor_tensor(newton[:, :], newton[:, :], var[:, :], ALU.mult))
                link(nc.vector.tensor_scalar(newton[:, :], newton[:, :], -0.5, 1.5, ALU.mult, ALU.add))
                link(nc.vector.tensor_tensor(rstd[:, :], rstd[:, :], newton[:, :], ALU.mult))
                for q in range(4):
                    t = slice(q * QT, (q + 1) * QT)
                    nc.vector.tensor_tensor(xall[:, t, :], xall[:, t, :],
                                            rstd[:, t].unsqueeze(2).to_broadcast((P, QT, F)),
                                            ALU.mult).then_inc(h_ready, 1)
                with dve.Fori(0, GROUPS // 2) as i:
                    for k in range(2):
                        b = i * 2 + k
                        dve.wait_ge(wh_mm, b + (L * GROUPS + 1))
                        got = psum[:, 2 + k, 0:GT * (F + 2)].rearrange("p (t f) -> p t f", t=GT)
                        t = bass.ds(b * GT, GT)
                        nc.vector.tensor_copy(wh[:, t, 0:F], got[:, :, 0:F])
                        nc.vector.tensor_copy(sd[:, t, :], got[:, :, F:F + 2]).then_inc(wh_free, 1)
                dve.wait_ge(wh_free, 2 + (L + 1) * GROUPS)
                nc.vector.tensor_reduce(cmax[:, 3:4], sd[:, :, 1], AX.X, ALU.max).then_inc(dmax_part, 1)
                nc.vector.tensor_reduce(whsum[:, :], wh[:, :, 0:F].rearrange("p t f -> p f t"), AX.X,
                                        ALU.add).then_inc(whsum_ready, 1)
                nc.vector.tensor_scalar(steep_d[:, :], sd[:, :, 1], STEEP, 1.0, ALU.mult, ALU.add)
                dve.wait_ge(dmax_ready, L + 1)
                nc.vector.tensor_scalar(cmax[:, 1:2], cmax[:, 0:1], -1.0, None, ALU.mult)
                nc.vector.tensor_scalar(cmax[:, 2:3], cmax[:, 0:1], -LEAK, None, ALU.mult)
                link(nc.vector.tensor_scalar(zc[:, 0, :], sd[:, :, 0], cmax[:, 0:1], None, ALU.add))
                link(nc.vector.tensor_scalar(zc[:, 1, :], zc[:, 0, :], LEAK, None, ALU.mult))
                link(nc.vector.tensor_tensor(newton[:, :], zc[:, 0, :], zc[:, 1, :], ALU.max))
                nc.vector.tensor_tensor(zc[:, 2, :], zc[:, 0, :], newton[:, :], ALU.subtract)
                nc.vector.tensor_tensor(zc[:, 3, :], zc[:, 1, :], newton[:, :], ALU.subtract).then_inc(exp_in, 1)
                dve.wait_ge(exp_ready, L + 1)
                with dve.Fori(0, SPLITS // 2) as i:
                    for k in range(2):
                        t = bass.ds((i * 2 + k) * SB, SB)
                        dve.wait_ge(parts_ready[0], i * 2 + (L * SPLITS + 2))
                        nc.vector.tensor_tensor(rest[:, 0, k, :, :], wh[:, t, :],
                                                dg[:, 0, t].unsqueeze(2).to_broadcast((P, SB, H)),
                                                ALU.mult).then_inc(scaled[0], 1)
                    for k in range(2):
                        t = bass.ds((i * 2 + k) * SB, SB)
                        dve.wait_ge(hi_ready[0], i * 2 + (L * SPLITS + k + 1))
                        nc.vector.tensor_tensor(rest[:, 0, k, :, :], rest[:, 0, k, :, :], parts[:, t, 0, 0, :],
                                                ALU.subtract).then_inc(rest1[0], 1)
                    for k in range(2):
                        t = bass.ds((i * 2 + k) * SB, SB)
                        dve.wait_ge(mid_ready[0], i * 2 + (L * SPLITS + k + 1))
                        nc.vector.tensor_tensor(parts[:, t, 0, 2, :], rest[:, 0, k, :, :], parts[:, t, 0, 1, :],
                                                ALU.subtract).then_inc(parts_ready[0], 1)
                dve.wait_ge(parts_ready[1], (L + 1) * SPLITS + 2)
                dve.wait_ge(parts_ready[0], (L + 1) * SPLITS + 2)

            def convert(g, s):
                step = g * GSTEPS + s
                dve.wait_ge(stage_in[s % 4], (g * (GSTEPS // 4) + (s // 4 + 1)) * 16)
                dve.wait_ge(packed, step + 1)
                nc.vector.tensor_scalar(natural[:, 1, :], stage[:, s % 4, :], 0, None, ALU.is_gt).then_inc(conv[1], 1)

            def store_words(g, k):
                r = g * GT + k
                dve.wait_ge(packed, (r + 1) * STEPS + 2)
                nc.vector.tensor_copy(words[:, :, bass.ds(r * WPT, WPT)],
                                      psum[:, 4 + k % 2, 0:TILES * WPT].rearrange("p (t w) -> p t w", t=TILES)
                                      ).then_inc(stored, 1)

            def unpack(L, g, u):
                n = (g + L * GROUPS) * CHUNKS + u * CPU
                if not (isinstance(g, int) and L + g + u == 0):
                    dve.wait_ge(chunk_used, n)
                w = words[:, u * UT:(u + 1) * UT, bass.ds(g * (GT * WPT), GT * WPT)].rearrange(
                    "p t (k m) -> p t k m", k=GT)
                b_out = bits[:, u % 2, :, :].rearrange("p t (k b m) -> p t k b m", k=GT, b=BITS)
                for b in range(BITS):
                    up = 14 - b
                    ins = nc.vector.tensor_scalar(
                        b_out[:, :, :, b, :], w, abs(up), MARK,
                        ALU.logical_shift_left if up >= 0 else ALU.logical_shift_right, ALU.bitwise_and)
                ins.then_inc(unpacked, 1)

            def masks(L, g, c, between):
                n = (g + L * GROUPS) * CHUNKS + c
                edge = bits[:, (c // CPU) % 2, (c % CPU) * CT:(c % CPU + 1) * CT, :].rearrange(
                    "p j i -> p (j i)").bitcast(I32)
                pos = tog[:, c % TOG, :, :].rearrange("p j i -> p (j i)").bitcast(I32)
                dve.wait_ge(sign_ready, n + 1)
                if c % CPU == 0:
                    dve.wait_ge(unpacked, (g + L * GROUPS) * UNPACKS + c // CPU + 1)
                nc.vector.tensor_tensor(pos, edge, pos, ALU.bitwise_and).then_inc(anded, 1)
                between()
                dve.wait_ge(anded, n + 1)
                nc.vector.tensor_tensor(edge, edge, pos, ALU.bitwise_xor).then_inc(masks_ready, 1)

            def invert_den(L, g):
                dve.wait_ge(den_ready, g + (L * GROUPS + 1))
                nc.vector.reciprocal(rden[:, :, :], den[:, :, :]).then_inc(den_inv, 1)

            def invert_half(L, g):
                dve.wait_ge(half_ready, g + (L * GROUPS + 1))
                nc.vector.reciprocal(hneg[:, :, :], hneg[:, :, :]).then_inc(half_inv, 1)

            def group(L, g, packing, first):
                if L == 0:
                    dve.wait_ge(stored, g * GT + (GT + 2))
                for c in range(CHUNKS):
                    if c % CPU == 0:
                        unpack(L, g, c // CPU)

                    def between():
                        if packing:
                            for s in steps_at(c):
                                if s % 2 == 1:
                                    convert(g + 1, s)
                            for k in words_at(c):
                                store_words(g + 1, k)
                    masks(L, g, c, between)
                    if not first:
                        if c == 4:
                            invert_den(L, g - 1)
                        if c == CHUNKS - 1:
                            invert_half(L, g - 1)

            constants()
            prepare(0)
            for k in range(GT):
                for s in range(k * STEPS + 1, (k + 1) * STEPS, 2):
                    convert(0, s)
                store_words(0, k)
            group(0, 0, True, True)
            with dve.Fori(1, GROUPS - 1) as g:
                group(0, g, True, False)
            group(0, GROUPS - 1, False, False)
            invert_den(0, GROUPS - 1)
            invert_half(0, GROUPS - 1)
            prepare(1)
            group(1, 0, False, True)
            with dve.Fori(1, GROUPS) as g:
                group(1, g, False, False)
            invert_den(1, GROUPS - 1)
            invert_half(1, GROUPS - 1)

        @block.tensor
        def _(pe):
            pe.sem_inc(packed, 2)
            pe.sem_inc(chunk_used, TOG)

            def constants():
                pe.wait_ge(const_in, 96)
                pe.wait_ge(const_pool, 2)
                for l in range(2):
                    ins = nc.tensor.transpose(psum[0:F, 0, l * F:(l + 1) * F], wrow[:, l, :], ident[0:F, 0:F])
                ins.then_inc(const_pe, 1)
                pe.wait_ge(const_dve, 3)
                nc.tensor.matmul(psum[0:F, 1, 0:2], wcol[:, 0, :], acol[:, 0, :], start=True, stop=True)
                nc.tensor.matmul(psum[0:F, 1, 2:4], wrow[:, 1, :], acol[:, 1, :], start=True, stop=True
                                 ).then_inc(const_pe, 1)
                pe.wait_ge(const_dve, 4)

            def prepare(L):
                for q in range(4):
                    pe.wait_ge(h_ready, q + (4 * L + 1))

                    def turn(k):
                        for j in range(GT):
                            t = q * QT + (k * GT + j)
                            ins = nc.tensor.transpose(psum[0:F, k % 2, j * P:(j + 1) * P],
                                                      xall[:, t, :],
                                                      ident[:, :])
                        ins.then_inc(turned, 1)

                    def project(k):
                        b = q * QB + (L * GROUPS + k)
                        pe.wait_ge(ht_ready, b + 1)
                        pe.wait_ge(srow_free, b + 1)
                        nc.tensor.matmul(psum[0:1, 6 + k % 2, :], waug[:, L, F:F + 1], ht[:, k % 2, :],
                                         start=True, stop=True).then_inc(s_mm, 1)
                        pe.wait_ge(wh_free, b + 1)
                        for j in range(GT):
                            ins = nc.tensor.matmul(psum[:, 2 + k % 2, j * (F + 2):(j + 1) * (F + 2)],
                                                   ht[:, k % 2, j * P:(j + 1) * P], waug[:, L, :],
                                                   start=True, stop=True)
                        ins.then_inc(wh_mm, 1)

                    turn(0)
                    for k in range(QB):
                        if k + 1 < QB:
                            turn(k + 1)
                        project(k)
                pe.wait_ge(whsum_ready, L + 1)
                pe.wait_ge(srow_free, 2 + (L + 1) * GROUPS)
                nc.tensor.matmul(psum[:, 7, 0:F], ones[:, :], whsum[:, :], start=True, stop=True
                                 ).then_inc(whmean_mm, 1)

            def pack(g, s):
                step = g * GSTEPS + s
                k = s // STEPS
                pe.wait_ge(conv[s % 2], (step - s % 2) // 2 + 3)
                if s % STEPS == 0:
                    pe.wait_ge(stored, g * GT + k + 1)
                for j in range(LT):
                    t = (s % STEPS) * LT + j
                    ins = nc.tensor.matmul(psum[:, 4 + k % 2, t * WPT:(t + 1) * WPT],
                                           natural[:, s % 2, j * P:(j + 1) * P], pack_w[:, :],
                                           start=True, stop=True)
                ins.then_inc(packed, 1)

            def group(L, g, packing):
                gg = g + L * GROUPS
                for c in range(CHUNKS):
                    n = gg * CHUNKS + c
                    if packing:
                        for s in steps_at(c):
                            pack(g + 1, s)
                    pe.wait_ge(masks_ready, n + 1)
                    for r in range(GT):
                        if c == 0:
                            pe.wait_ge(bank_free, gg * GT + r + 1)
                            nc.tensor.matmul(psum[:, r, 0:2 * W3], zero_w[:, :], parts[:, 0, :, :, :].rearrange(
                                "p e k h -> p (e k h)"), start=True, stop=False, skip_group_check=True)
                        for j in range(CT):
                            t = c * CT + j
                            for e, mask in ((0, tog[:, c % TOG, j, r * P:(r + 1) * P]),
                                            (1, bits[:, (c // CPU) % 2, (c % CPU) * CT + j, r * P:(r + 1) * P])):
                                ins = nc.tensor.matmul(psum[:, r, e * W3:(e + 1) * W3], mask.bitcast(BF16),
                                                       parts[:, t, e, :, :].rearrange("p k h -> p (k h)"),
                                                       start=False, stop=(c == CHUNKS - 1 and j == CT - 1),
                                                       skip_group_check=True)
                        if c == CHUNKS - 1 and r < GT - 1:
                            ins.then_inc(bank_done, 1)
                    if c == CHUNKS - 1:
                        ins.then_inc(chunk_used, 1)
                        pe.wait_ge(chunk_used, n + 1 + TOG)
                        pe.sem_inc(bank_done, 1)
                    else:
                        ins.then_inc(chunk_used, 1)

            constants()
            prepare(0)
            for s in range(GSTEPS):
                pack(0, s)
            for L in range(2):
                if L == 1:
                    prepare(1)
                for e in range(2):
                    pe.wait_ge(parts_ready[e], (L + 1) * SPLITS + 2)
                if L == 0:
                    with pe.Fori(0, GROUPS - 1) as g:
                        group(0, g, True)
                    group(0, GROUPS - 1, False)
                else:
                    with pe.Fori(0, GROUPS) as g:
                        group(1, g, False)


_INS = ["x", "adj", "L0_gnn_W", "L0_gnn_a", "L1_gnn_W", "L1_gnn_a"]


def kernel(**inputs):
    import concourse.bacc as _bacc
    from concourse import mybir as _mybir
    from concourse.bass_utils import run_bass_kernel_spmd as _run

    nc = _bacc.Bacc("TRN2", target_bir_lowering=False, num_devices=1)
    arrays, args = {}, []
    for name in _INS:
        a = np.ascontiguousarray(inputs[name])
        arrays[f"in_{name}_dram"] = a
        args.append(nc.dram_tensor(f"in_{name}_dram", a.shape, _mybir.dt.from_np(a.dtype), kind="ExternalInput").ap())
    args.append(nc.dram_tensor("out_dram", inputs["x"].shape, _mybir.dt.float32, kind="ExternalOutput").ap())
    gat2_kernel(nc, *args)
    r = _run(nc, [arrays], core_ids=[0])
    return r.results[0]["out_dram"]
```

```python
from contextlib import ExitStack

import numpy as np
import concourse.bass as bass
from concourse import mybir

ALU = mybir.AluOpType
ACT = mybir.ActivationFunctionType
AX = mybir.AxisListType
F32 = mybir.dt.float32
BF16 = mybir.dt.bfloat16
FP8 = mybir.dt.float8e4
I32 = mybir.dt.int32
U16 = mybir.dt.uint16
U8 = mybir.dt.uint8

P = 128
LEAK = 0.2
EPS = 1e-5
BITS = 16
MARK = 0x40
MARKS = 0x4040
STEEP = 1e20
ONE8 = 0x38


def gat2_kernel(nc, x, adj, w0, a0, w1, a1, out):
    N, F = x.shape
    TILES = N // P
    GT = 4
    GROUP = GT * P
    GROUPS = N // GROUP
    CT = 8
    CHUNKS = TILES // CT
    UT = min(32, TILES // 2)
    UNPACKS = TILES // UT
    CPU = UT // CT
    WPT = P // BITS
    LW = 1024
    LT = LW // P
    STEPS = N // LW
    GSTEPS = GT * STEPS
    PACE = GSTEPS // CHUNKS
    AHEAD = 2 * PACE
    NAT = 4
    DVE_SIGNS = (0, 2)
    H = F + 1
    W3 = 3 * H
    QT = TILES // 4
    QB = QT // GT
    SB = 8
    SPLITS = TILES // SB
    TOG = 4
    ALL = 2 * GSTEPS
    assert UNPACKS % 2 == 0 and CHUNKS % TOG == 0

    def steps_at(c, limit):
        return [s for s in range(AHEAD + c * PACE, AHEAD + (c + 1) * PACE) if s < limit]

    def words_at(c, limit):
        done = [s + 1 for s in range(AHEAD + (c - 1) * PACE, AHEAD + c * PACE) if (s + 1) % STEPS == 0]
        return [d // STEPS - 1 for d in done if d <= limit]

    with ExitStack() as ctx:
        def sb(name, shape, dt):
            return ctx.enter_context(nc.sbuf_tensor(name, shape, dt))

        def sem(name):
            return ctx.enter_context(nc.semaphore(name))

        x1 = nc.dram_tensor("x1_scratch", (N, F), F32)
        s_dram = nc.dram_tensor("s_scratch", (2, N), F32)
        psum = ctx.enter_context(nc.psum_tensor("psum", [P, 8, 512], F32))

        words = sb("words", [P, TILES, N // BITS], U16)
        parts = sb("parts", [P, TILES, 2, 3, H], BF16)
        work = sb("work", [P, 2 * UT * GROUP], U8)
        toggle = sb("toggle", [P, TOG * CT * GROUP], U8)
        stage = sb("stage", [P, 4, LW], I32)
        natural = sb("natural", [P, NAT, LW], U8)
        s_row = sb("s_row", [P, 2, GROUP], F32)
        sums = sb("sums", [P, GT, 6, H], F32)
        sum3 = sb("sum3", [P, GT, 3, H], F32)
        x_tile = sb("x_tile", [P, GT, F], F32)
        y_tile = sb("y_tile", [P, GT, F], F32)
        hneg = sb("hneg", [P, GT, F], F32)
        th = sb("th", [P, GT, F], F32)
        tmp = sb("tmp", [P, GT, F], F32)
        flag = sb("flag", [P, GT, 1], F32)
        den = sb("den", [P, GT, 1], F32)
        rden = sb("rden", [P, GT, 1], F32)
        ident = sb("ident", [P, P], F32)
        pack_w = sb("pack_w", [P, WPT], BF16)
        zero_w = sb("zero_w", [P, P], BF16)
        wrow = sb("wrow", [F, 2, F], F32)
        wcol = sb("wcol", [F, 2, F], F32)
        acol = sb("acol", [F, 2, 2], F32)
        waug = sb("waug", [F, 2, F + 2], F32)
        ones = sb("ones", [P, P], F32)
        mean = sb("mean", [P, TILES], F32)
        var = sb("var", [P, TILES], F32)
        std = sb("std", [P, TILES], F32)
        rstd = sb("rstd", [P, TILES], F32)
        newton = sb("newton", [P, TILES], F32)
        sd = sb("sd", [P, TILES, 2], F32)
        dg = sb("dg", [P, 2, TILES], F32)
        uv = sb("uv", [P, 2, TILES], F32)
        steep_d = sb("steep_d", [P, TILES], F32)
        zc = sb("zc", [P, 4, TILES], F32)
        cmax = sb("cmax", [P, 4], F32)
        whsum = sb("whsum", [P, F], F32)
        whmean = sb("whmean", [P, F], F32)
        minus_d = sb("minus_d", [P, TILES], F32)

        bits = work.rearrange("p (s j i) -> p s j i", s=2, j=UT)
        tog = toggle.rearrange("p (s j i) -> p s j i", s=TOG, j=CT)
        xall = toggle[:, 0:4 * TILES * F].bitcast(F32).rearrange("p (t f) -> p t f", t=TILES)
        work_f = work[:, :].bitcast(F32)
        wh = work_f[:, 0:TILES * H].rearrange("p (t h) -> p t h", t=TILES)
        o = TILES * H
        rest = work_f[:, o:o + 4 * SB * H].rearrange("p (b s t h) -> p b s t h", b=2, s=2, t=SB)
        o += 4 * SB * H
        ht = work_f[0:F, o:o + 2 * GROUP].rearrange("p (s i) -> p s i", s=2)
        square = work_f[:, 0:QT * F].rearrange("p (t f) -> p t f", t=QT)
        srow_sb = sums[0:1, :, :, :].rearrange("p a b c -> p (a b c)")[:, 0:2 * GROUP].rearrange(
            "p (s i) -> p s i", s=2)
        hot = sums[:, :, :, :].rearrange("p a b c -> p (a b c)")[:, 0:P]
        power = sums[:, :, :, :].rearrange("p a b c -> p (a b c)")[:, P:2 * P]
        packing_sum = sums[:, :, :, :].rearrange("p a b c -> p (a b c)")[:, 2 * P:2 * P + WPT]

        const_in = sem("const_in")
        const_pool = sem("const_pool")
        const_dve = sem("const_dve")
        apart = sem("apart")
        const_pe = sem("const_pe")
        x_in = [sem(f"x_in{q}") for q in range(4)]
        chain = sem("chain")
        var_ready = sem("var_ready")
        std_ready = sem("std_ready")
        h_ready = sem("h_ready")
        turned = sem("turned")
        ht_ready = sem("ht_ready")
        s_mm = sem("s_mm")
        wh_mm = sem("wh_mm")
        wh_free = sem("wh_free")
        srow_free = sem("srow_free")
        s_stored = [sem("s_stored0"), sem("s_stored1")]
        dmax_part = sem("dmax_part")
        dmax_ready = sem("dmax_ready")
        exp_in = sem("exp_in")
        exp_ready = sem("exp_ready")
        whsum_ready = sem("whsum_ready")
        whmean_mm = sem("whmean_mm")
        whmean_ready = sem("whmean_ready")
        scaled = [sem("scaled_dve"), sem("scaled_pool")]
        hi_ready = [sem("hi_dve"), sem("hi_pool")]
        rest1 = [sem("rest1_dve"), sem("rest1_pool")]
        mid_ready = [sem("mid_dve"), sem("mid_pool")]
        parts_ready = [sem("parts_dve"), sem("parts_pool")]
        stage_in = [sem(f"stage_in{s}") for s in range(4)]
        conv = sem("conv")
        packed = sem("packed")
        stored = sem("stored")
        row_in = sem("row_in")
        sign_ready = sem("sign_ready")
        signs_dve = sem("signs_dve")
        chunk_used = sem("chunk_used")
        unpacked = sem("unpacked")
        anded = sem("anded")
        masks_ready = sem("masks_ready")
        bank_done = sem("bank_done")
        bank_free = sem("bank_free")
        sums_free = sem("sums_free")
        neg_ready = sem("neg_ready")
        tanh_ready = sem("tanh_ready")
        den_ready = sem("den_ready")
        den_inv = sem("den_inv")
        half_ready = sem("half_ready")
        half_inv = sem("half_inv")
        pool_step = sem("pool_step")
        xt_in = sem("xt_in")
        y_stored = sem("y_stored")

        def settled(eng):
            eng.sem_inc(apart, 1)

        adj_t = adj.rearrange("(r p) (l w) -> r p l w", p=P, w=LW)
        block = ctx.enter_context(nc.Block())
        src_of = [x, x1[:, :]]
        dst_of = [x1[:, :], out]

        @block.sync
        def _(sp):
            sp.dma_start(wrow[:, 0, :], w0).then_inc(const_in, 16)
            sp.dma_start(wrow[:, 1, :], w1).then_inc(const_in, 16)
            for k in range(2):
                sp.dma_start(acol[:, 0, k:k + 1], a0[k * F:(k + 1) * F, :]).then_inc(const_in, 16)
                sp.dma_start(acol[:, 1, k:k + 1], a1[k * F:(k + 1) * F].unsqueeze(1)).then_inc(const_in, 16)

            def load_x(L):
                src = src_of[L].rearrange("(t p) f -> p t f", p=P)
                for q in range(4):
                    sp.dma_start(xall[:, q * QT:(q + 1) * QT, :], src[:, q * QT:(q + 1) * QT, :]).then_inc(x_in[q], 16)

            def store_s(L):
                with sp.Fori(0, GROUPS // 2) as i:
                    for par in range(2):
                        b = i * 2 + par
                        sp.wait_ge(srow_free, b + (L * GROUPS + 3))
                        sp.dma_start(s_dram[L:L + 1, bass.ds(b * GROUP, GROUP)],
                                     srow_sb[:, par, :]).then_inc(s_stored[par], 16)

            def load_adj(row_tile, first_step, steps=range(STEPS)):
                for s in steps:
                    slot = s % 4
                    sp.wait_ge(conv, first_step + (s + 1))
                    sp.dma_start(stage[:, slot, :], adj_t[bass.ds(row_tile, 1), :, s, :].rearrange("r p w -> (r p) w")
                                 ).then_inc(stage_in[slot], 16)

            def load_row(L, g):
                gg = g + L * GROUPS
                if not (isinstance(g, int) and g + L == 0):
                    sp.wait_ge(row_in, gg * 16)
                sp.dma_start(s_row[:, g % 2, :] if isinstance(g, int) else s_row[:, bass.ds(g % 2, 1), :].rearrange("p o i -> p (o i)"),
                             s_dram[L:L + 1, bass.ds(g * GROUP, GROUP)].to_broadcast((P, GROUP))).then_inc(row_in, 16)

            load_x(0)
            load_adj(0, 0, range(4))
            store_s(0)
            load_adj(0, 0, range(4, STEPS))
            with sp.Fori(1, GT) as r:
                load_adj(r, r * STEPS)
            for par in range(2):
                sp.wait_ge(s_stored[par], 16 * (GROUPS // 2 + 1))
            load_row(0, 0)
            load_row(0, 1)
            for k in range(GT):
                load_adj(GT + k, (GT + k) * STEPS)
            with sp.Fori(2, GROUPS) as g:
                for k in range(GT):
                    load_adj(g * GT + k, (g * GT + k) * STEPS)
                    if k == GT // 2:
                        sp.wait_ge(masks_ready, (g - 1) * CHUNKS)
                        settled(sp)
                        load_row(0, g)

            sp.wait_ge(y_stored, 16 * GROUPS)
            sp.wait_ge(chunk_used, TOG + GROUPS * CHUNKS)
            load_x(1)
            store_s(1)
            for par in range(2):
                sp.wait_ge(s_stored[par], 16 * (GROUPS + 1))
            load_row(1, 0)
            load_row(1, 1)
            with sp.Fori(2, GROUPS) as g:
                sp.wait_ge(masks_ready, (g + GROUPS - 1) * CHUNKS)
                settled(sp)
                load_row(1, g)

        @block.scalar
        def _(act):
            act.sem_inc(stored, 2)
            act.sem_inc(srow_free, 2)
            act.sem_inc(bank_free, GT)
            for par in range(2):
                act.sem_inc(s_stored[par], 16)

            def prepare(L):
                act.wait_ge(var_ready, L + 1)
                nc.scalar.activation(std[:, :], var[:, :], ACT.Sqrt).then_inc(std_ready, 1)
                with act.Fori(0, 4) as q:
                    for k in range(QB):
                        b = q * QB + (L * GROUPS + k)
                        act.wait_ge(turned, b + 1)
                        nc.scalar.activation(ht[:, k % 2, :], psum[0:F, k % 2, :], ACT.Relu).then_inc(ht_ready, 1)
                        act.wait_ge(s_mm, b + 1)
                        act.wait_ge(s_stored[k % 2], (q * (QB // 2) + ((L * GROUPS + k) // 2 + 1)) * 16)
                        nc.scalar.copy(srow_sb[:, k % 2, :], psum[0:1, 6 + k % 2, :]).then_inc(srow_free, 1)
                act.wait_ge(exp_in, L + 1)
                nc.scalar.activation(dg[:, 0, :], sd[:, :, 1], ACT.Exp, bias=cmax[:, 1:2])
                nc.scalar.activation(dg[:, 1, :], sd[:, :, 1], ACT.Exp, bias=cmax[:, 2:3], scale=LEAK)
                nc.scalar.activation(uv[:, 0, :], zc[:, 2, :], ACT.Exp)
                nc.scalar.activation(uv[:, 1, :], zc[:, 3, :], ACT.Exp).then_inc(exp_ready, 1)
                with act.Fori(0, SPLITS // 2) as i:
                    for part, have, done in ((0, scaled, hi_ready), (1, rest1, mid_ready)):
                        for k in range(2):
                            for e in range(2):
                                act.wait_ge(have[e], i * 2 + (L * SPLITS + k + 1))
                                settled(act)
                                nc.scalar.copy(parts[:, bass.ds((i * 2 + k) * SB, SB), e, part, :],
                                               rest[:, e, k, :, :]).then_inc(done[e], 1)
                act.wait_ge(whmean_mm, L + 1)
                nc.scalar.mul(whmean[:, :], psum[:, 7, 0:F], 1.0 / N).then_inc(whmean_ready, 1)

            def store_words(g, k):
                r = g * GT + k
                act.wait_ge(packed, (r + 1) * STEPS + NAT)
                settled(act)
                nc.scalar.copy(words[:, :, bass.ds(r * WPT, WPT)],
                               psum[:, 4 + k % 2, 0:TILES * WPT].rearrange("p (t w) -> p t w", t=TILES)
                               ).then_inc(stored, 1)

            def signs(L, g, c):
                n = (g + L * GROUPS) * CHUNKS + c
                act.wait_ge(chunk_used, n + 1)
                slot = g % 2
                row = s_row[:, slot, :] if isinstance(g, int) else s_row[:, bass.ds(slot, 1), :].rearrange("p o i -> p (o i)")
                settled(act)
                for j in range(CT - DVE_SIGNS[L]):
                    t = c * CT + j
                    ins = nc.scalar.activation(tog[:, c % TOG, j, :], row, ACT.Relu,
                                               scale=STEEP, bias=steep_d[:, t:t + 1])
                ins.then_inc(sign_ready, 1)

            def take_sums(L, g):
                gg = g + L * GROUPS
                act.wait_ge(sums_free, gg + 1)
                for r in range(GT):
                    act.wait_ge(bank_done, gg * GT + r + 1)
                    settled(act)
                    for e in range(2):
                        ins = nc.scalar.activation(sums[:, r, 3 * e:3 * e + 3, :].rearrange("p k h -> p (k h)"),
                                                   psum[:, r, e * W3:(e + 1) * W3], ACT.Copy,
                                                   scale=uv[:, e, bass.ds(g * GT + r, 1)])
                    ins.then_inc(bank_free, 1)

            def tanh(L, g):
                gg = g + L * GROUPS
                act.wait_ge(neg_ready, gg + 1)
                nc.scalar.activation(th[:, :, :], hneg[:, :, :], ACT.Tanh, scale=0.5).then_inc(tanh_ready, 1)

            def group(L, g, limit, first):
                act.wait_ge(row_in, (g + L * GROUPS + 1) * 16)
                for c in range(CHUNKS):
                    signs(L, g, c)
                    for k in words_at(c, limit):
                        store_words(g + 1, k)
                    if not first:
                        if c == 1:
                            take_sums(L, g - 1)
                        if c == 3:
                            tanh(L, g - 1)

            act.wait_ge(const_dve, 2)
            prepare(0)
            for k in range(GT):
                store_words(0, k)
            group(0, 0, ALL, True)
            with act.Fori(1, GROUPS - 2) as g:
                group(0, g, ALL, False)
            group(0, GROUPS - 2, GSTEPS, False)
            group(0, GROUPS - 1, 0, False)
            take_sums(0, GROUPS - 1)
            tanh(0, GROUPS - 1)
            prepare(1)
            group(1, 0, 0, True)
            with act.Fori(1, GROUPS) as g:
                group(1, g, 0, False)
            take_sums(1, GROUPS - 1)
            tanh(1, GROUPS - 1)

        @block.gpsimd
        def _(pool):
            pool.sem_inc(sums_free, 1)
            pool.sem_inc(parts_ready[1], 2)
            nc.gpsimd.memset(ident[:, :], 0.0).then_inc(const_pool, 1)
            pool.wait_ge(const_pool, 1)
            nc.gpsimd.affine_select(out=ident[:, :], in_=ident[:, :], compare_op=ALU.not_equal, fill=1.0, base=0,
                                    pattern=[[-1, P]], channel_multiplier=1).then_inc(const_pool, 1)

            def split(L):
                pool.wait_ge(exp_ready, L + 1)
                with pool.Fori(0, SPLITS // 2) as i:
                    for k in range(2):
                        t = bass.ds((i * 2 + k) * SB, SB)
                        pool.wait_ge(parts_ready[1], i * 2 + (L * SPLITS + 2))
                        settled(pool)
                        nc.gpsimd.tensor_tensor(rest[:, 1, k, :, :], wh[:, t, :],
                                                dg[:, 1, t].unsqueeze(2).to_broadcast((P, SB, H)),
                                                ALU.mult).then_inc(scaled[1], 1)
                    for k in range(2):
                        t = bass.ds((i * 2 + k) * SB, SB)
                        pool.wait_ge(hi_ready[1], i * 2 + (L * SPLITS + k + 1))
                        nc.gpsimd.tensor_tensor(rest[:, 1, k, :, :], rest[:, 1, k, :, :], parts[:, t, 1, 0, :],
                                                ALU.subtract).then_inc(rest1[1], 1)
                    for k in range(2):
                        t = bass.ds((i * 2 + k) * SB, SB)
                        pool.wait_ge(mid_ready[1], i * 2 + (L * SPLITS + k + 1))
                        nc.gpsimd.tensor_tensor(parts[:, t, 1, 2, :], rest[:, 1, k, :, :], parts[:, t, 1, 1, :],
                                                ALU.subtract).then_inc(parts_ready[1], 1)

            STEP = 10

            def finish(L, g):
                gg = g + L * GROUPS
                done = [0]

                def link(ins):
                    done[0] += 1
                    ins.then_inc(pool_step, 1)
                    pool.wait_ge(pool_step, gg * STEP + done[0])
                    settled(pool)

                src = src_of[L].rearrange("(t p) f -> p t f", p=P)
                dst = dst_of[L].rearrange("(t p) f -> p t f", p=P)
                settled(pool)
                pool.dma_start(x_tile[:, :, :], src[:, bass.ds(g * GT, GT), :]).then_inc(xt_in, 16)
                pool.wait_ge(bank_free, (gg + 1) * GT + GT)
                link(nc.gpsimd.tensor_tensor(sum3[:, :, :, :], sums[:, :, 0:3, :], sums[:, :, 3:6, :], ALU.add))
                pool.sem_inc(sums_free, 1)
                link(nc.gpsimd.tensor_tensor(sum3[:, :, 1, :], sum3[:, :, 1, :], sum3[:, :, 2, :], ALU.add))
                link(nc.gpsimd.tensor_tensor(sum3[:, :, 0, :], sum3[:, :, 0, :], sum3[:, :, 1, :], ALU.add))
                link(nc.gpsimd.tensor_scalar(flag[:, :, :], sum3[:, :, 0, F:H], 0.0, None, ALU.is_equal))
                nc.gpsimd.tensor_tensor(den[:, :, :], sum3[:, :, 0, F:H], flag[:, :, :], ALU.add).then_inc(den_ready, 1)
                link(nc.gpsimd.tensor_tensor(tmp[:, :, :], flag[:, :, :].to_broadcast((P, GT, F)),
                                             whmean[:, :].unsqueeze(1).to_broadcast((P, GT, F)), ALU.mult))
                link(nc.gpsimd.tensor_tensor(tmp[:, :, :], tmp[:, :, :], sum3[:, :, 0, 0:F], ALU.add))
                pool.wait_ge(den_inv, gg + 1)
                settled(pool)
                link(nc.gpsimd.tensor_tensor(tmp[:, :, :], tmp[:, :, :],
                                             rden[:, :, :].to_broadcast((P, GT, F)), ALU.mult))
                nc.gpsimd.tensor_scalar(hneg[:, :, :], tmp[:, :, :], 0.0, None, ALU.min).then_inc(neg_ready, 1)
                pool.wait_ge(tanh_ready, gg + 1)
                settled(pool)
                nc.gpsimd.tensor_scalar(hneg[:, :, :], th[:, :, :], -0.5, 0.5, ALU.mult, ALU.add).then_inc(half_ready, 1)
                pool.wait_ge(half_inv, gg + 1)
                link(nc.gpsimd.tensor_tensor(hneg[:, :, :], th[:, :, :], hneg[:, :, :], ALU.mult))
                nc.gpsimd.tensor_scalar(tmp[:, :, :], tmp[:, :, :], 0.0, None, ALU.max)
                pool.wait_ge(xt_in, (gg + 1) * 16)
                link(nc.gpsimd.tensor_tensor(hneg[:, :, :], hneg[:, :, :], x_tile[:, :, :], ALU.add))
                link(nc.gpsimd.tensor_tensor(y_tile[:, :, :], hneg[:, :, :], tmp[:, :, :], ALU.add))
                assert done[0] == STEP, done[0]
                pool.dma_start(dst[:, bass.ds(g * GT, GT), :], y_tile[:, :, :]).then_inc(y_stored, 16)
                pool.wait_ge(y_stored, (gg + 1) * 16)

            for L in range(2):
                pool.wait_ge(dmax_part, L + 1)
                nc.gpsimd.partition_all_reduce(cmax[:, 0:1], cmax[:, 3:4], P,
                                               bass.bass_isa.ReduceOp.max).then_inc(dmax_ready, 1)
                split(L)
                pool.wait_ge(whmean_ready, L + 1)
                with pool.Fori(0, GROUPS) as g:
                    finish(L, g)

        @block.vector
        def _(dve):
            dve.sem_inc(conv, 4)
            dve.sem_inc(wh_free, 2)
            dve.sem_inc(parts_ready[0], 2)
            links = [0]

            def link(ins):
                links[0] += 1
                ins.then_inc(chain, 1)
                dve.wait_ge(chain, links[0])

            def constants():
                nc.vector.memset(ones[:, :], 1.0)
                nc.vector.memset(zero_w[:, :], 0.0).then_inc(const_dve, 1)
                by_bit = power.rearrange("p (b w e) -> p b w e", b=8, w=WPT)
                for b in range(8):
                    for e in range(2):
                        ins = nc.vector.memset(by_bit[:, b, :, e], float(2 ** (b + 8 * e)))
                link(ins)
                dve.wait_ge(const_pool, 2)
                link(nc.vector.tensor_tensor(hot, ident[:, :], power, ALU.mult))
                link(nc.vector.tensor_reduce(packing_sum, hot.rearrange("p (b w e) -> p w b e", b=8, w=WPT), AX.XY,
                                             ALU.add))
                nc.vector.tensor_copy(pack_w[:, :], packing_sum).then_inc(const_dve, 1)
                dve.wait_ge(const_pe, 1)
                nc.vector.tensor_copy(wcol[:, :, :], psum[0:F, 0, 0:2 * F].rearrange("p (l f) -> p l f", l=2)
                                      ).then_inc(const_dve, 1)
                dve.wait_ge(const_pe, 2)
                nc.vector.tensor_copy(waug[:, :, F:F + 2], psum[0:F, 1, 0:4].rearrange("p (l k) -> p l k", l=2))
                nc.vector.tensor_copy(waug[:, 0, 0:F], wrow[:, 0, :])
                nc.vector.tensor_copy(waug[:, 1, 0:F], wcol[:, 1, :]).then_inc(const_dve, 1)

            def prepare(L):
                for q in range(4):
                    t = slice(q * QT, (q + 1) * QT)
                    dve.wait_ge(x_in[q], 16 * (L + 1))
                    link(nc.vector.tensor_reduce(mean[:, t], xall[:, t, :], AX.X, ALU.add))
                    link(nc.vector.tensor_scalar(mean[:, t], mean[:, t], -1.0 / F, None, ALU.mult))
                    link(nc.vector.tensor_tensor(xall[:, t, :], xall[:, t, :],
                                                 mean[:, t].unsqueeze(2).to_broadcast((P, QT, F)), ALU.add))
                    link(nc.vector.tensor_tensor(square[:, :, :], xall[:, t, :], xall[:, t, :], ALU.mult))
                    link(nc.vector.tensor_reduce(var[:, t], square[:, :, :], AX.X, ALU.add))
                link(nc.vector.tensor_scalar(var[:, :], var[:, :], 1.0 / F, EPS, ALU.mult, ALU.add))
                dve.sem_inc(var_ready, 1)
                nc.vector.memset(wh[:, :, F:H], 1.0)
                dve.wait_ge(std_ready, L + 1)
                link(nc.vector.reciprocal(rstd[:, :], std[:, :]))
                link(nc.vector.tensor_tensor(newton[:, :], rstd[:, :], rstd[:, :], ALU.mult))
                link(nc.vector.tensor_tensor(newton[:, :], newton[:, :], var[:, :], ALU.mult))
                link(nc.vector.tensor_scalar(newton[:, :], newton[:, :], -0.5, 1.5, ALU.mult, ALU.add))
                link(nc.vector.tensor_tensor(rstd[:, :], rstd[:, :], newton[:, :], ALU.mult))
                for q in range(4):
                    t = slice(q * QT, (q + 1) * QT)
                    nc.vector.tensor_tensor(xall[:, t, :], xall[:, t, :],
                                            rstd[:, t].unsqueeze(2).to_broadcast((P, QT, F)),
                                            ALU.mult).then_inc(h_ready, 1)
                with dve.Fori(0, GROUPS // 2) as i:
                    for k in range(2):
                        b = i * 2 + k
                        dve.wait_ge(wh_mm, b + (L * GROUPS + 1))
                        got = psum[:, 2 + k, 0:GT * (F + 2)].rearrange("p (t f) -> p t f", t=GT)
                        t = bass.ds(b * GT, GT)
                        nc.vector.tensor_copy(wh[:, t, 0:F], got[:, :, 0:F])
                        nc.vector.tensor_copy(sd[:, t, :], got[:, :, F:F + 2]).then_inc(wh_free, 1)
                dve.wait_ge(wh_free, 2 + (L + 1) * GROUPS)
                nc.vector.tensor_reduce(cmax[:, 3:4], sd[:, :, 1], AX.X, ALU.max).then_inc(dmax_part, 1)
                nc.vector.tensor_reduce(whsum[:, :], wh[:, :, 0:F].rearrange("p t f -> p f t"), AX.X,
                                        ALU.add).then_inc(whsum_ready, 1)
                nc.vector.tensor_scalar(minus_d[:, :], sd[:, :, 1], -1.0, None, ALU.mult)
                nc.vector.tensor_scalar(steep_d[:, :], sd[:, :, 1], STEEP, None, ALU.mult)
                dve.wait_ge(dmax_ready, L + 1)
                nc.vector.tensor_scalar(cmax[:, 1:2], cmax[:, 0:1], -1.0, None, ALU.mult)
                nc.vector.tensor_scalar(cmax[:, 2:3], cmax[:, 0:1], -LEAK, None, ALU.mult)
                link(nc.vector.tensor_scalar(zc[:, 0, :], sd[:, :, 0], cmax[:, 0:1], None, ALU.add))
                link(nc.vector.tensor_scalar(zc[:, 1, :], zc[:, 0, :], LEAK, None, ALU.mult))
                link(nc.vector.tensor_tensor(newton[:, :], zc[:, 0, :], zc[:, 1, :], ALU.max))
                nc.vector.tensor_tensor(zc[:, 2, :], zc[:, 0, :], newton[:, :], ALU.subtract)
                nc.vector.tensor_tensor(zc[:, 3, :], zc[:, 1, :], newton[:, :], ALU.subtract).then_inc(exp_in, 1)
                dve.wait_ge(exp_ready, L + 1)
                with dve.Fori(0, SPLITS // 2) as i:
                    for k in range(2):
                        t = bass.ds((i * 2 + k) * SB, SB)
                        dve.wait_ge(parts_ready[0], i * 2 + (L * SPLITS + 2))
                        nc.vector.tensor_tensor(rest[:, 0, k, :, :], wh[:, t, :],
                                                dg[:, 0, t].unsqueeze(2).to_broadcast((P, SB, H)),
                                                ALU.mult).then_inc(scaled[0], 1)
                    for k in range(2):
                        t = bass.ds((i * 2 + k) * SB, SB)
                        dve.wait_ge(hi_ready[0], i * 2 + (L * SPLITS + k + 1))
                        nc.vector.tensor_tensor(rest[:, 0, k, :, :], rest[:, 0, k, :, :], parts[:, t, 0, 0, :],
                                                ALU.subtract).then_inc(rest1[0], 1)
                    for k in range(2):
                        t = bass.ds((i * 2 + k) * SB, SB)
                        dve.wait_ge(mid_ready[0], i * 2 + (L * SPLITS + k + 1))
                        nc.vector.tensor_tensor(parts[:, t, 0, 2, :], rest[:, 0, k, :, :], parts[:, t, 0, 1, :],
                                                ALU.subtract).then_inc(parts_ready[0], 1)
                dve.wait_ge(parts_ready[1], (L + 1) * SPLITS + 2)
                dve.wait_ge(parts_ready[0], (L + 1) * SPLITS + 2)

            def convert(g, s):
                step = g * GSTEPS + s
                dve.wait_ge(stage_in[s % 4], (g * (GSTEPS // 4) + (s // 4 + 1)) * 16)
                dve.wait_ge(packed, step + 1)
                nc.vector.tensor_scalar(natural[:, s % NAT, :], stage[:, s % 4, :], 0, float(ONE8),
                                        ALU.is_gt, ALU.mult).then_inc(conv, 1)

            def unpack(L, g, u):
                n = (g + L * GROUPS) * CHUNKS + u * CPU
                if not (isinstance(g, int) and L + g + u == 0):
                    dve.wait_ge(chunk_used, n)
                w = words[:, u * UT:(u + 1) * UT, bass.ds(g * (GT * WPT), GT * WPT)].rearrange(
                    "p t (k m) -> p t k m", k=GT)
                b_out = work[:, (u % 2) * UT * GROUP:(u % 2 + 1) * UT * GROUP].bitcast(U16).rearrange(
                    "p (t k b m) -> p t k b m", t=UT, k=GT, b=8)
                for b in range(8):
                    up = 6 - b
                    ins = nc.vector.tensor_scalar(
                        b_out[:, :, :, b, :], w, abs(up), MARKS,
                        ALU.logical_shift_left if up >= 0 else ALU.logical_shift_right, ALU.bitwise_and)
                ins.then_inc(unpacked, 1)

            def masks(L, g, c, between):
                n = (g + L * GROUPS) * CHUNKS + c
                edge = bits[:, (c // CPU) % 2, (c % CPU) * CT:(c % CPU + 1) * CT, :].rearrange(
                    "p j i -> p (j i)").bitcast(I32)
                pos = tog[:, c % TOG, :, :].rearrange("p j i -> p (j i)").bitcast(I32)
                if DVE_SIGNS[L]:
                    dve.wait_ge(chunk_used, n + 1)
                    dve.wait_ge(row_in, (g + L * GROUPS + 1) * 16)
                    row = s_row[:, g % 2, :] if isinstance(g, int) else s_row[:, bass.ds(g % 2, 1), :].rearrange("p o i -> p (o i)")
                    for j in range(CT - DVE_SIGNS[L], CT):
                        t = c * CT + j
                        ins = nc.vector.tensor_scalar(tog[:, c % TOG, j, :], row, minus_d[:, t:t + 1], float(MARK),
                                                      ALU.is_gt, ALU.mult)
                    ins.then_inc(signs_dve, 1)
                    dve.wait_ge(signs_dve, (g + (L - 1) * GROUPS) * CHUNKS + c + 1)
                dve.wait_ge(sign_ready, n + 1)
                if c % CPU == 0:
                    dve.wait_ge(unpacked, (g + L * GROUPS) * UNPACKS + c // CPU + 1)
                nc.vector.tensor_tensor(pos, edge, pos, ALU.bitwise_and).then_inc(anded, 1)
                between()
                dve.wait_ge(anded, n + 1)
                nc.vector.tensor_tensor(edge, edge, pos, ALU.bitwise_xor).then_inc(masks_ready, 1)

            def invert_den(L, g):
                dve.wait_ge(den_ready, g + (L * GROUPS + 1))
                nc.vector.reciprocal(rden[:, :, :], den[:, :, :]).then_inc(den_inv, 1)

            def invert_half(L, g):
                dve.wait_ge(half_ready, g + (L * GROUPS + 1))
                nc.vector.reciprocal(hneg[:, :, :], hneg[:, :, :]).then_inc(half_inv, 1)

            def group(L, g, limit, first):
                if L == 0:
                    dve.wait_ge(stored, g * GT + (GT + 2))
                for c in range(CHUNKS):
                    if c % CPU == 0:
                        unpack(L, g, c // CPU)

                    def between():
                        for s in steps_at(c, limit):
                            convert(g + 1, s)
                    masks(L, g, c, between)
                    if not first:
                        if c == 2:
                            invert_den(L, g - 1)
                        if c == CHUNKS - 1:
                            invert_half(L, g - 1)

            constants()
            prepare(0)
            for s in range(GSTEPS + AHEAD):
                convert(0, s)
            group(0, 0, ALL, True)
            with dve.Fori(1, GROUPS - 2) as g:
                group(0, g, ALL, False)
            group(0, GROUPS - 2, GSTEPS, False)
            group(0, GROUPS - 1, 0, False)
            invert_den(0, GROUPS - 1)
            invert_half(0, GROUPS - 1)
            prepare(1)
            group(1, 0, 0, True)
            with dve.Fori(1, GROUPS) as g:
                group(1, g, 0, False)
            invert_den(1, GROUPS - 1)
            invert_half(1, GROUPS - 1)

        @block.tensor
        def _(pe):
            pe.sem_inc(packed, NAT)
            pe.sem_inc(chunk_used, TOG)

            def constants():
                pe.wait_ge(const_in, 96)
                pe.wait_ge(const_pool, 2)
                for l in range(2):
                    ins = nc.tensor.transpose(psum[0:F, 0, l * F:(l + 1) * F], wrow[:, l, :], ident[0:F, 0:F])
                ins.then_inc(const_pe, 1)
                pe.wait_ge(const_dve, 3)
                nc.tensor.matmul(psum[0:F, 1, 0:2], wcol[:, 0, :], acol[:, 0, :], start=True, stop=True)
                nc.tensor.matmul(psum[0:F, 1, 2:4], wrow[:, 1, :], acol[:, 1, :], start=True, stop=True
                                 ).then_inc(const_pe, 1)
                pe.wait_ge(const_dve, 4)

            def prepare(L):
                for q in range(4):
                    pe.wait_ge(h_ready, q + (4 * L + 1))

                    def turn(k):
                        for j in range(GT):
                            t = q * QT + (k * GT + j)
                            ins = nc.tensor.transpose(psum[0:F, k % 2, j * P:(j + 1) * P],
                                                      xall[:, t, :],
                                                      ident[:, :])
                        ins.then_inc(turned, 1)

                    def project(k):
                        b = q * QB + (L * GROUPS + k)
                        pe.wait_ge(ht_ready, b + 1)
                        pe.wait_ge(srow_free, b + 1)
                        nc.tensor.matmul(psum[0:1, 6 + k % 2, :], waug[:, L, F:F + 1], ht[:, k % 2, :],
                                         start=True, stop=True).then_inc(s_mm, 1)
                        pe.wait_ge(wh_free, b + 1)
                        for j in range(GT):
                            ins = nc.tensor.matmul(psum[:, 2 + k % 2, j * (F + 2):(j + 1) * (F + 2)],
                                                   ht[:, k % 2, j * P:(j + 1) * P], waug[:, L, :],
                                                   start=True, stop=True)
                        ins.then_inc(wh_mm, 1)

                    turn(0)
                    for k in range(QB):
                        if k + 1 < QB:
                            turn(k + 1)
                        project(k)
                pe.wait_ge(whsum_ready, L + 1)
                pe.wait_ge(srow_free, 2 + (L + 1) * GROUPS)
                nc.tensor.matmul(psum[:, 7, 0:F], ones[:, :], whsum[:, :], start=True, stop=True
                                 ).then_inc(whmean_mm, 1)

            def pack(g, s):
                step = g * GSTEPS + s
                k = s // STEPS
                pe.wait_ge(conv, step + 5)
                if s % STEPS == 0:
                    pe.wait_ge(stored, g * GT + k + 1)
                settled(pe)
                for j in range(LT):
                    t = (s % STEPS) * LT + j
                    ins = nc.tensor.matmul(psum[:, 4 + k % 2, t * WPT:(t + 1) * WPT],
                                           natural[:, s % NAT, j * P:(j + 1) * P].bitcast(FP8), pack_w[:, :],
                                           start=True, stop=True)
                ins.then_inc(packed, 1)

            def group(L, g, limit):
                gg = g + L * GROUPS
                for c in range(CHUNKS):
                    n = gg * CHUNKS + c
                    for s in steps_at(c, limit):
                        pack(g + 1, s)
                    pe.wait_ge(masks_ready, n + 1)
                    settled(pe)
                    for r in range(GT):
                        if c == 0:
                            pe.wait_ge(bank_free, gg * GT + r + 1)
                            nc.tensor.matmul(psum[:, r, 0:2 * W3], zero_w[:, :], parts[:, 0, :, :, :].rearrange(
                                "p e k h -> p (e k h)"), start=True, stop=False, skip_group_check=True)
                        for j in range(CT):
                            t = c * CT + j
                            for e, mask in ((0, tog[:, c % TOG, j, r * P:(r + 1) * P]),
                                            (1, bits[:, (c // CPU) % 2, (c % CPU) * CT + j, r * P:(r + 1) * P])):
                                ins = nc.tensor.matmul(psum[:, r, e * W3:(e + 1) * W3], mask.bitcast(FP8),
                                                       parts[:, t, e, :, :].rearrange("p k h -> p (k h)"),
                                                       start=False, stop=(c == CHUNKS - 1 and j == CT - 1),
                                                       skip_group_check=True)
                        if c == CHUNKS - 1 and r < GT - 1:
                            ins.then_inc(bank_done, 1)
                    if c == CHUNKS - 1:
                        ins.then_inc(chunk_used, 1)
                        pe.wait_ge(chunk_used, n + 1 + TOG)
                        pe.sem_inc(bank_done, 1)
                    else:
                        ins.then_inc(chunk_used, 1)

            constants()
            prepare(0)
            for s in range(GSTEPS + AHEAD):
                pack(0, s)
            for L in range(2):
                if L == 1:
                    prepare(1)
                for e in range(2):
                    pe.wait_ge(parts_ready[e], (L + 1) * SPLITS + 2)
                if L == 0:
                    with pe.Fori(0, GROUPS - 2) as g:
                        group(0, g, ALL)
                    group(0, GROUPS - 2, GSTEPS)
                    group(0, GROUPS - 1, 0)
                else:
                    with pe.Fori(0, GROUPS) as g:
                        group(1, g, 0)


_INS = ["x", "adj", "L0_gnn_W", "L0_gnn_a", "L1_gnn_W", "L1_gnn_a"]


def kernel(**inputs):
    import concourse.bacc as _bacc
    from concourse import mybir as _mybir
    from concourse.bass_utils import run_bass_kernel_spmd as _run

    nc = _bacc.Bacc("TRN2", target_bir_lowering=False, num_devices=1)
    arrays, args = {}, []
    for name in _INS:
        a = np.ascontiguousarray(inputs[name])
        arrays[f"in_{name}_dram"] = a
        args.append(nc.dram_tensor(f"in_{name}_dram", a.shape, _mybir.dt.from_np(a.dtype), kind="ExternalInput").ap())
    args.append(nc.dram_tensor("out_dram", inputs["x"].shape, _mybir.dt.float32, kind="ExternalOutput").ap())
    gat2_kernel(nc, *args)
    r = _run(nc, [arrays], core_ids=[0])
    return r.results[0]["out_dram"]
```

```python
from contextlib import ExitStack

import numpy as np
import concourse.bass as bass
from concourse import mybir

ALU = mybir.AluOpType
ACT = mybir.ActivationFunctionType
AX = mybir.AxisListType
F32 = mybir.dt.float32
BF16 = mybir.dt.bfloat16
FP16 = mybir.dt.float16
FP8 = mybir.dt.float8e4
I32 = mybir.dt.int32
U16 = mybir.dt.uint16
U8 = mybir.dt.uint8

P = 128
LEAK = 0.2
EPS = 1e-5
BITS = 16
MARK = 0x40
MARKS = 0x4040
STEEP = 1e20
ONE8 = 0x38
SPREAD = 12.0
TALL = 16.0
TINY = 1e-35
FAR = 1e30


def gat2_kernel(nc, x, adj, w0, a0, w1, a1, out):
    N, F = x.shape
    TILES = N // P
    GT = 4
    GROUP = GT * P
    GROUPS = N // GROUP
    CT = 8
    CHUNKS = TILES // CT
    UT = 16
    UNPACKED = 4
    UNPACKS = TILES // UT
    CPU = UT // CT
    WPT = P // BITS
    LW = 1024
    LT = LW // P
    STEPS = N // LW
    GSTEPS = GT * STEPS
    PACE = GSTEPS // CHUNKS
    AHEAD = 2 * PACE
    NAT = 8
    DVE_SIGNS = 2
    H = F + 1
    PARTS = 2
    COLS = (0, 2 * H, 4 * H)
    TOP = 2.0 ** 14
    QT = TILES // 4
    QB = QT // GT
    SB = 8
    SPLITS = TILES // SB
    TOG = 4
    UNSHARED = (GROUPS - 1) * CHUNKS
    EARLY = 3
    SPANS = (((0, 4),), ((0, EARLY), (EARLY, 4)))
    TURN = (0, 4)
    PROJ = (2, 6)
    ALL = 2 * GSTEPS
    assert GSTEPS == 2 * GROUPS and NAT == 8 and AHEAD == 8
    assert UNPACKS % UNPACKED == 0 and CHUNKS % TOG == 0

    def steps_at(c, limit):
        return [s for s in range(AHEAD + c * PACE, AHEAD + (c + 1) * PACE) if s < limit]

    def words_at(c, limit):
        done = [s + 1 for s in range(AHEAD + (c - 2) * PACE, AHEAD + (c - 1) * PACE) if (s + 1) % STEPS == 0]
        return [d // STEPS - 1 for d in done if d <= limit]

    def shared(L, g):
        return L == 1 or isinstance(g, int) and g == GROUPS - 1

    with ExitStack() as ctx:
        def sb(name, shape, dt):
            return ctx.enter_context(nc.sbuf_tensor(name, shape, dt))

        def sem(name):
            return ctx.enter_context(nc.semaphore(name))

        x1 = nc.dram_tensor("x1_scratch", (N, F), F32)
        s_dram = nc.dram_tensor("s_scratch", (2, N), F32)
        d_dram = nc.dram_tensor("d_scratch", (2, N), F32)
        y_general = nc.dram_tensor("y_general", (2, N, F), F32)
        psum = ctx.enter_context(nc.psum_tensor("psum", [P, 8, 512], F32))

        words = sb("words", [P, TILES, N // BITS], U16)
        parts = (sb("parts_d", [P, TILES, PARTS, H], FP16),
                 sb("parts_g", [P, TILES, PARTS, H], FP16))
        work = sb("work", [P, UNPACKED * UT * GROUP], U8)
        toggle = sb("toggle", [P, TOG * CT * GROUP], U8)
        stage = sb("stage", [P, 4, LW], I32)
        natural = sb("natural", [P, NAT, LW], U8)
        s_row = sb("s_row", [P, 2, GROUP], F32)
        sums = sb("sums", [P, GT, 2 * PARTS, H], F32)
        sum2 = sb("sum2", [P, GT, 2, H], F32)
        x_tile = sb("x_tile", [P, GT, F], F32)
        y_tile = sb("y_tile", [P, GT, F], F32)
        hneg = sb("hneg", [P, GT, F], F32)
        th = sb("th", [P, GT, F], F32)
        ex = sb("ex", [P, GT, F], F32)
        tmp = sb("tmp", [P, GT, F], F32)
        flag = sb("flag", [P, GT, 1], F32)
        den = sb("den", [P, GT, 1], F32)
        rden = sb("rden", [P, GT, 1], F32)
        ident = sb("ident", [P, P], F32)
        pack_w = sb("pack_w", [P, WPT], BF16)
        zero_w = sb("zero_w", [P, COLS[2]], BF16)
        wrow = sb("wrow", [F, 2, F], F32)
        wcol = sb("wcol", [F, 2, F], F32)
        acol = sb("acol", [F, 2, 2], F32)
        waug = sb("waug", [P, 2, 2, F + 2], F32)
        ones = sb("ones", [P, P], F32)
        mean = sb("mean", [P, TILES], F32)
        var = sb("var", [P, TILES], F32)
        std = sb("std", [P, TILES], F32)
        rstd = sb("rstd", [P, TILES], F32)
        newton = sb("newton", [P, TILES], F32)
        sd = sb("sd", [P, TILES, 2], F32)
        dg = sb("dg", [P, 2, TILES], F32)
        uv = sb("uv", [P, 2, TILES], F32)
        steep_d = sb("steep_d", [P, TILES], F32)
        zc = sb("zc", [P, 4, TILES], F32)
        tops = sb("tops", [P, 3], F32)
        top = sb("top", [P, 3], F32)
        block_top = sb("block_top", [P, GROUPS], F32)
        beyond = sb("beyond", [P, 2], F32)
        unsafe = sb("unsafe", [P, 2], I32)
        shift = sb("shift", [P, 4], F32)
        whsum = sb("whsum", [P, F], F32)
        whmean = sb("whmean", [P, F], F32)
        minus_d = sb("minus_d", [P, TILES], F32)

        bits = work.rearrange("p (s j i) -> p s j i", s=UNPACKED, j=UT)
        tog = toggle.rearrange("p (s j i) -> p s j i", s=TOG, j=CT)
        xall = (toggle[:, 0:4 * TILES * F].bitcast(F32).rearrange("p (t f) -> p t f", t=TILES),
                stage.rearrange("p s w -> p (s w)")[:, 0:TILES * F].bitcast(F32).rearrange("p (t f) -> p t f", t=TILES))
        work_f = work[:, :].bitcast(F32)
        wh = work_f[:, 0:TILES * F].rearrange("p (t f) -> p t f", t=TILES)
        o = TILES * F
        rest = work_f[:, o:o + 4 * SB * F].rearrange("p (b s t f) -> p b s t f", b=2, s=2, t=SB)
        o += 4 * SB * F
        ht = work_f[:, o:o + 2 * 2 * P].rearrange("p (s i) -> p s i", s=2)
        spare = natural.rearrange("p s w -> p (s w)").bitcast(F32).rearrange("p (t f) -> p t f", f=F)
        square = ([work_f[:, q * QT * F:(q + 1) * QT * F].rearrange("p (t f) -> p t f", t=QT) for q in range(4)],
                  [spare[:, (q % 2) * QT:(q % 2 + 1) * QT, :] for q in range(4)])
        s_turned = sums[0:TILES, :, :, :].rearrange("p a b c -> p (a b c)")[:, 0:P]
        hot = sums[:, :, :, :].rearrange("p a b c -> p (a b c)")[:, 0:P]
        power = sums[:, :, :, :].rearrange("p a b c -> p (a b c)")[:, P:2 * P]
        packing_sum = sums[:, :, :, :].rearrange("p a b c -> p (a b c)")[:, 2 * P:2 * P + WPT]

        LC = 8
        vlow = toggle[:, :].bitcast(F32).rearrange("p (c j) -> p c j", j=LW)
        vhigh = work_f[:, TILES * F:2 * TILES * F].rearrange("p (c j) -> p c j", j=LW)
        scores = [vlow[:, c, :] if c < LC // 2 else vhigh[:, c - LC // 2, :] for c in range(LC)]
        nat = natural.rearrange("p s w -> p (s w)")
        adj_chunk = nat[:, 0:4 * LW].bitcast(I32)
        masked_d = nat[:, 0:4 * LW].bitcast(F32)
        d_row = nat[:, 4 * LW:8 * LW].bitcast(F32)
        leaked = d_row
        probs_t = masked_d.rearrange("p (t i) -> p t i", t=LT)
        small = sums[:, :, :, :].rearrange("p a b c -> p (a b c)")
        d_turned = small[0:TILES, P:2 * P]
        chunk_max = small[:, 2 * P:2 * P + LC]
        chunk_sum = small[:, 2 * P + LC:2 * P + 2 * LC]
        col = [small[:, 3 * P + k:3 * P + k + 1] for k in range(6)]
        s_cur, row_max, row_leak, minus_max, row_sum, row_inv = col
        x_gen = tmp[:, 0, :]
        y_gen = y_tile[:, 0, :]

        const_in = sem("const_in")
        const_pool = sem("const_pool")
        const_dve = sem("const_dve")
        waug_twice = sem("waug_twice")
        apart = sem("apart")
        const_pe = sem("const_pe")
        x_in = [sem(f"x_in{q}") for q in range(4)]
        chain = sem("chain")
        centred = sem("centred")
        squared = sem("squared")
        var_sums = sem("var_sums")
        squares_used = sem("squares_used")
        var_ready = sem("var_ready")
        std_ready = sem("std_ready")
        turned = sem("turned")
        ht_ready = sem("ht_ready")
        wh_mm = sem("wh_mm")
        s_turn = sem("s_turn")
        s_copied = sem("s_copied")
        s_stored = sem("s_stored")
        factors = sem("factors")
        wh_free = sem("wh_free")
        tops_found = sem("tops_found")
        dmax_part = sem("dmax_part")
        dmax_ready = sem("dmax_ready")
        exp_in = sem("exp_in")
        exp_ready = sem("exp_ready")
        whmean_mm = sem("whmean_mm")
        whmean_ready = sem("whmean_ready")
        scaled = [sem("scaled_dve"), sem("scaled_pool")]
        hi_ready = [sem("hi_dve"), sem("hi_pool")]
        parts_ready = [sem("parts_dve"), sem("parts_pool")]
        stage_in = [sem(f"stage_in{s}") for s in range(4)]
        conv = sem("conv")
        packed = sem("packed")
        stored = sem("stored")
        row_in = sem("row_in")
        sign_ready = sem("sign_ready")
        signs_dve = sem("signs_dve")
        chunk_used = sem("chunk_used")
        unpacked = sem("unpacked")
        anded = sem("anded")
        masks_ready = sem("masks_ready")
        bank_done = sem("bank_done")
        bank_free = sem("bank_free")
        sums_free = sem("sums_free")
        neg_ready = sem("neg_ready")
        tanh_ready = sem("tanh_ready")
        den_ready = sem("den_ready")
        den_inv = sem("den_inv")
        pool_step = sem("pool_step")
        xt_in = sem("xt_in")
        y_stored = sem("y_stored")

        def pair(name):
            return [sem(f"{name}_{l}") for l in range(2)]

        unsafe_ready = sem("unsafe_ready")
        gen_d_turn = pair("gen_d_turn")
        gen_d_copied = pair("gen_d_copied")
        gen_d_stored = pair("gen_d_stored")
        gen_x_in = pair("gen_x_in")
        gen_in = pair("gen_in")
        gen_masked = pair("gen_masked")
        gen_scores = pair("gen_scores")
        gen_probs = pair("gen_probs")
        gen_turned = pair("gen_turned")
        gen_lhs = pair("gen_lhs")
        gen_mm = pair("gen_mm")
        gen_neg = pair("gen_neg")
        gen_tanh = pair("gen_tanh")
        gen_y = pair("gen_y")
        gen_y_stored = pair("gen_y_stored")
        gen_fixed = pair("gen_fixed")
        gen_step = pair("gen_step")

        def when_unsafe(eng, L, body):
            eng.wait_ge(unsafe_ready, L + 1)
            flag_value = eng.value_load(unsafe[0:1, L:L + 1], min_val=0, max_val=2)
            with eng.If(flag_value > 0):
                body()

        def settled(eng):
            eng.sem_inc(apart, 1)

        adj_t = adj.rearrange("(r p) (l w) -> r p l w", p=P, w=LW)
        block = ctx.enter_context(nc.Block())
        src_of = [x, x1[:, :]]
        dst_of = [x1[:, :], out]

        @block.sync
        def _(sp):
            sp.dma_start(wrow[:, 0, :], w0).then_inc(const_in, 16)
            sp.dma_start(wrow[:, 1, :], w1).then_inc(const_in, 16)
            for k in range(2):
                sp.dma_start(acol[:, 0, k:k + 1], a0[k * F:(k + 1) * F, :]).then_inc(const_in, 16)
                sp.dma_start(acol[:, 1, k:k + 1], a1[k * F:(k + 1) * F].unsqueeze(1)).then_inc(const_in, 16)

            def load_x(L, q0, q1):
                src = src_of[L].rearrange("(t p) f -> p t f", p=P)
                for q in range(q0, q1):
                    sp.dma_start(xall[L][:, q * QT:(q + 1) * QT, :], src[:, q * QT:(q + 1) * QT, :]).then_inc(x_in[q], 16)

            def store_s(L):
                sp.wait_ge(s_copied, L + 1)
                sp.dma_start(s_dram[L].rearrange("(t p) -> t p", p=P), s_turned).then_inc(s_stored, 16)
                sp.wait_ge(s_stored, 16 * (L + 1))

            def load_adj(row_tile, first_step, steps=range(STEPS)):
                for s in steps:
                    slot = s % 4
                    sp.wait_ge(conv, first_step + (s + 1))
                    sp.dma_start(stage[:, slot, :], adj_t[bass.ds(row_tile, 1), :, s, :].rearrange("r p w -> (r p) w")
                                 ).then_inc(stage_in[slot], 16)

            def load_row(L, g):
                gg = g + L * GROUPS
                if not (isinstance(g, int) and g + L == 0):
                    sp.wait_ge(row_in, gg * 16)
                sp.dma_start(s_row[:, g % 2, :] if isinstance(g, int) else s_row[:, bass.ds(g % 2, 1), :].rearrange("p o i -> p (o i)"),
                             s_dram[L:L + 1, bass.ds(g * GROUP, GROUP)].to_broadcast((P, GROUP))).then_inc(row_in, 16)

            def general(L):
                sp.wait_ge(gen_d_copied[L], 1)
                sp.dma_start(d_dram[L].rearrange("(t p) -> t p", p=P), d_turned).then_inc(gen_d_stored[L], 16)
                sp.wait_ge(gen_d_stored[L], 16)
                with sp.Fori(0, TILES) as r:
                    sp.dma_start(x_gen, src_of[L].rearrange("(t p) f -> t p f", p=P)[bass.ds(r, 1)]
                                 .rearrange("t p f -> (t p) f")).then_inc(gen_x_in[L], 16)
                    for c in range(LC):
                        sp.wait_ge(gen_masked[L], r * LC + (c + 1))
                        settled(sp)
                        sp.dma_start(adj_chunk, adj_t[bass.ds(r, 1), :, c, :].rearrange("r p w -> (r p) w")
                                     ).then_inc(gen_in[L], 16)
                        sp.dma_start(d_row, d_dram[L:L + 1, c * LW:(c + 1) * LW].to_broadcast((P, LW))
                                     ).then_inc(gen_in[L], 16)
                    sp.wait_ge(gen_y[L], r + 1)
                    settled(sp)
                    sp.dma_start(y_general[L].rearrange("(t p) f -> t p f", p=P)[bass.ds(r, 1)]
                                 .rearrange("t p f -> (t p) f"), y_gen).then_inc(gen_y_stored[L], 16)
                    sp.wait_ge(gen_y_stored[L], (r + 1) * 16)
                    settled(sp)

            def replace(L, q0, q1, nth):
                rows = slice(q0 * QT * P, q1 * QT * P)
                sp.dma_start(dst_of[L][rows, :], y_general[L][rows, :]).then_inc(gen_fixed[L], 16)
                sp.wait_ge(gen_fixed[L], 16 * nth)

            load_x(0, 0, 4)
            load_adj(0, 0, range(4))
            sp.wait_ge(const_dve, 4)
            sp.dma_start(waug[F:2 * F, :, 1, :], waug[0:F, :, 0, :]).then_inc(waug_twice, 16)
            load_adj(0, 0, range(4, STEPS))
            with sp.Fori(1, GT) as r:
                load_adj(r, r * STEPS)
            load_adj(GT, GSTEPS)
            store_s(0)
            when_unsafe(sp, 0, lambda: general(0))
            load_row(0, 0)
            load_row(0, 1)
            for k in range(1, GT):
                load_adj(GT + k, (GT + k) * STEPS)
            with sp.Fori(2, GROUPS) as g:
                for k in range(GT):
                    load_adj(g * GT + k, (g * GT + k) * STEPS)
                    if k == GT // 2:
                        sp.wait_ge(masks_ready, (g - 1) * CHUNKS)
                        settled(sp)
                        load_row(0, g)

            sp.wait_ge(conv, GROUPS * GSTEPS + 4)
            sp.wait_ge(y_stored, 16 * EARLY * QB)
            when_unsafe(sp, 0, lambda: replace(0, 0, EARLY, 1))
            load_x(1, 0, EARLY)
            sp.wait_ge(y_stored, 16 * GROUPS)
            when_unsafe(sp, 0, lambda: replace(0, EARLY, 4, 2))
            load_x(1, EARLY, 4)
            store_s(1)
            when_unsafe(sp, 1, lambda: general(1))
            load_row(1, 0)
            load_row(1, 1)
            with sp.Fori(2, GROUPS) as g:
                sp.wait_ge(masks_ready, (g + GROUPS - 1) * CHUNKS)
                settled(sp)
                load_row(1, g)
            sp.wait_ge(y_stored, 2 * 16 * GROUPS)
            when_unsafe(sp, 1, lambda: replace(1, 0, 4, 1))

        @block.scalar
        def _(act):
            act.sem_inc(stored, 2)
            act.sem_inc(bank_free, GT)

            def store_words(g, k):
                r = g * GT + k
                act.wait_ge(packed, (r + 1) * STEPS + NAT)
                settled(act)
                nc.scalar.copy(words[:, :, bass.ds(r * WPT, WPT)],
                               psum[:, 4 + k % 2, 0:TILES * WPT].rearrange("p (t w) -> p t w", t=TILES)
                               ).then_inc(stored, 1)

            def normalise(L, span):
                q0, q1 = SPANS[L][span]
                t = slice(q0 * QT, q1 * QT)
                for q in range(q0, q1):
                    act.wait_ge(centred, 4 * L + q + 1)
                    if q >= q0 + 2 and L == 1:
                        act.wait_ge(squares_used, q - 1)
                    nc.scalar.activation(square[L][q], xall[L][:, q * QT:(q + 1) * QT, :], ACT.Square
                                         ).then_inc(squared, 1)
                act.wait_ge(var_ready, L + span + 1)
                nc.scalar.activation(std[:, t], var[:, t], ACT.Sqrt).then_inc(std_ready, 1)

            def rectify(L, b0, b1):
                for b in range(b0, b1):
                    act.wait_ge(turned, L * GROUPS + b + 1)
                    nc.scalar.activation(ht[:, b % 2, :], psum[:, TURN[L] + b % 2, 0:2 * P], ACT.Relu
                                         ).then_inc(ht_ready, 1)
                    if L == 0 and b % 4 == 3:
                        store_words(0, b // 4)

            def prepare(L):
                act.wait_ge(s_turn, L + 1)
                nc.scalar.copy(s_turned, psum[0:TILES, TURN[L], 0:P]).then_inc(s_copied, 1)
                act.wait_ge(exp_in, L + 1)
                nc.scalar.activation(dg[:, 0, :], sd[:, :, 1], ACT.Exp, bias=shift[:, 0:1])
                nc.scalar.activation(dg[:, 1, :], sd[:, :, 1], ACT.Exp, bias=shift[:, 1:2], scale=LEAK)
                nc.scalar.activation(uv[:, 0, :], zc[:, 2, :], ACT.Exp)
                nc.scalar.activation(uv[:, 1, :], zc[:, 3, :], ACT.Exp).then_inc(exp_ready, 1)

                def cast(i, k, e, part, have, done):
                    act.wait_ge(have, i * 2 + (L * SPLITS + k + 1))
                    settled(act)
                    nc.scalar.copy(parts[e][:, bass.ds((i * 2 + k) * SB, SB), part, 0:F],
                                   rest[:, e, k, :, :]).then_inc(done, 1)

                with act.Fori(0, SPLITS // 2) as i:
                    for k in range(2):
                        cast(i, k, 0, 0, scaled[0], hi_ready[0])
                        cast(i, k, 1, 0, scaled[1], hi_ready[1])

            def general(L):
                act.wait_ge(gen_d_turn[L], 1)
                nc.scalar.copy(d_turned, psum[0:TILES, TURN[L] + 1, 0:P]).then_inc(gen_d_copied[L], 1)
                with act.Fori(0, TILES) as r:
                    for c in range(LC):
                        act.wait_ge(gen_scores[L], r * LC + (c + 1))
                        settled(act)
                        nc.scalar.activation(scores[c], scores[c], ACT.Exp, bias=minus_max).then_inc(gen_probs[L], 1)
                    for c in range(LC):
                        act.wait_ge(gen_turned[L], r * LC + (c + 1))
                        act.wait_ge(gen_mm[L], r * LC + (c + 1))
                        settled(act)
                        nc.scalar.copy(probs_t, psum[:, 0:2, :].rearrange("p b (t i) -> p (b t) i", i=P)
                                       ).then_inc(gen_lhs[L], 1)
                    act.wait_ge(gen_neg[L], r + 1)
                    settled(act)
                    nc.scalar.activation(th[:, 0, :], hneg[:, 0, :], ACT.Tanh, scale=0.5).then_inc(gen_tanh[L], 1)
                act.wait_ge(gen_y[L], TILES)

            def signs(L, g, c):
                n = (g + L * GROUPS) * CHUNKS + c
                act.wait_ge(chunk_used, n + 1)
                slot = g % 2
                row = s_row[:, slot, :] if isinstance(g, int) else s_row[:, bass.ds(slot, 1), :].rearrange("p o i -> p (o i)")
                settled(act)
                for j in range(CT - DVE_SIGNS if shared(L, g) else CT):
                    t = c * CT + j
                    ins = nc.scalar.activation(tog[:, c % TOG, j, :], row, ACT.Relu,
                                               scale=STEEP, bias=steep_d[:, t:t + 1])
                ins.then_inc(sign_ready, 1)

            def take_sums(L, g):
                gg = g + L * GROUPS
                act.wait_ge(sums_free, gg + 1)
                for r in range(GT):
                    act.wait_ge(bank_done, gg * GT + r + 1)
                    settled(act)
                    for e in range(2):
                        ins = nc.scalar.activation(sums[:, r, PARTS * e:PARTS * (e + 1), :].rearrange("p k h -> p (k h)"),
                                                   psum[:, r, COLS[e]:COLS[e + 1]], ACT.Copy,
                                                   scale=uv[:, e, bass.ds(g * GT + r, 1)])
                    ins.then_inc(bank_free, 1)

            def tanh(L, g):
                gg = g + L * GROUPS
                act.wait_ge(neg_ready, gg + 1)
                nc.scalar.activation(th[:, :, :], hneg[:, :, :], ACT.Tanh, scale=0.5)
                nc.scalar.activation(ex[:, :, :], hneg[:, :, :], ACT.Exp).then_inc(tanh_ready, 1)

            def group(L, g, limit, first):
                act.wait_ge(row_in, (g + L * GROUPS + 1) * 16)
                for c in range(CHUNKS):
                    signs(L, g, c)
                    for k in words_at(c, limit):
                        store_words(g + 1, k)
                    if not first:
                        if c == 1:
                            take_sums(L, g - 1)
                        if c == 5:
                            tanh(L, g - 1)

            act.wait_ge(const_dve, 2)
            normalise(0, 0)
            rectify(0, 0, GROUPS)
            prepare(0)
            when_unsafe(act, 0, lambda: general(0))
            group(0, 0, ALL, True)
            with act.Fori(1, GROUPS - 2) as g:
                group(0, g, ALL, False)
            group(0, GROUPS - 2, GSTEPS, False)
            group(0, GROUPS - 1, 0, False)
            take_sums(0, GROUPS - 1)
            normalise(1, 0)
            rectify(1, 0, 1)
            tanh(0, GROUPS - 1)
            rectify(1, 1, EARLY * QB)
            normalise(1, 1)
            rectify(1, EARLY * QB, GROUPS)
            prepare(1)
            when_unsafe(act, 1, lambda: general(1))
            group(1, 0, 0, True)
            with act.Fori(1, GROUPS) as g:
                group(1, g, 0, False)
            take_sums(1, GROUPS - 1)
            tanh(1, GROUPS - 1)

        @block.gpsimd
        def _(pool):
            pool.sem_inc(sums_free, 1)
            pool.sem_inc(parts_ready[1], 2)
            nc.gpsimd.memset(ident[:, :], 0.0).then_inc(const_pool, 1)
            pool.wait_ge(const_pool, 1)
            nc.gpsimd.affine_select(out=ident[:, :], in_=ident[:, :], compare_op=ALU.not_equal, fill=1.0, base=0,
                                    pattern=[[-1, P]], channel_multiplier=1).then_inc(const_pool, 1)

            def split(L):
                pool.wait_ge(factors, L + 1)
                with pool.Fori(0, SPLITS // 2) as i:
                    pool.wait_ge(parts_ready[1], i * 2 + (L * SPLITS + 2))
                    settled(pool)
                    for k in range(2):
                        t = bass.ds((i * 2 + k) * SB, SB)
                        nc.gpsimd.tensor_tensor(rest[:, 1, k, :, :], wh[:, t, :],
                                                dg[:, 1, t].unsqueeze(2).to_broadcast((P, SB, F)),
                                                ALU.mult).then_inc(scaled[1], 1)
                    for k in range(2):
                        t = bass.ds((i * 2 + k) * SB, SB)
                        pool.wait_ge(hi_ready[1], i * 2 + (L * SPLITS + k + 1))
                        nc.gpsimd.tensor_tensor(parts[1][:, t, 1, 0:F], rest[:, 1, k, :, :], parts[1][:, t, 0, 0:F],
                                                ALU.subtract).then_inc(parts_ready[1], 1)

            STEP = 10

            def finish(L, g):
                gg = g + L * GROUPS
                done = [0]

                def link(ins):
                    done[0] += 1
                    ins.then_inc(pool_step, 1)
                    pool.wait_ge(pool_step, gg * STEP + done[0])
                    settled(pool)

                src = src_of[L].rearrange("(t p) f -> p t f", p=P)
                dst = dst_of[L].rearrange("(t p) f -> p t f", p=P)
                settled(pool)
                pool.dma_start(x_tile[:, :, :], src[:, bass.ds(g * GT, GT), :]).then_inc(xt_in, 16)
                pool.wait_ge(bank_free, (gg + 1) * GT + GT)
                link(nc.gpsimd.tensor_tensor(sum2[:, :, :, :], sums[:, :, 0:2, :], sums[:, :, 2:4, :], ALU.add))
                pool.sem_inc(sums_free, 1)
                link(nc.gpsimd.tensor_tensor(sum2[:, :, 0, :], sum2[:, :, 0, :], sum2[:, :, 1, :], ALU.add))
                link(nc.gpsimd.tensor_scalar(flag[:, :, :], sum2[:, :, 0, F:H], TINY, None, ALU.is_lt))
                nc.gpsimd.tensor_tensor(den[:, :, :], sum2[:, :, 0, F:H], flag[:, :, :], ALU.add).then_inc(den_ready, 1)
                link(nc.gpsimd.tensor_tensor(tmp[:, :, :], flag[:, :, :].to_broadcast((P, GT, F)),
                                             whmean[:, :].unsqueeze(1).to_broadcast((P, GT, F)), ALU.mult))
                link(nc.gpsimd.tensor_tensor(tmp[:, :, :], tmp[:, :, :], sum2[:, :, 0, 0:F], ALU.add))
                pool.wait_ge(den_inv, gg + 1)
                settled(pool)
                link(nc.gpsimd.tensor_tensor(tmp[:, :, :], tmp[:, :, :],
                                             rden[:, :, :].to_broadcast((P, GT, F)), ALU.mult))
                nc.gpsimd.tensor_scalar(hneg[:, :, :], tmp[:, :, :], 0.0, None, ALU.min).then_inc(neg_ready, 1)
                pool.wait_ge(tanh_ready, gg + 1)
                settled(pool)
                nc.gpsimd.tensor_scalar(tmp[:, :, :], tmp[:, :, :], 0.0, None, ALU.max)
                link(nc.gpsimd.tensor_scalar(ex[:, :, :], ex[:, :, :], 1.0, None, ALU.add))
                link(nc.gpsimd.tensor_tensor(hneg[:, :, :], th[:, :, :], ex[:, :, :], ALU.mult))
                pool.wait_ge(xt_in, (gg + 1) * 16)
                link(nc.gpsimd.tensor_tensor(hneg[:, :, :], hneg[:, :, :], x_tile[:, :, :], ALU.add))
                link(nc.gpsimd.tensor_tensor(y_tile[:, :, :], hneg[:, :, :], tmp[:, :, :], ALU.add))
                assert done[0] == STEP, done[0]
                pool.dma_start(dst[:, bass.ds(g * GT, GT), :], y_tile[:, :, :]).then_inc(y_stored, 16)
                pool.wait_ge(y_stored, (gg + 1) * 16)

            for L in range(2):
                pool.wait_ge(dmax_part, L + 1)
                nc.gpsimd.partition_all_reduce(top[:, :], tops[:, :], P,
                                               bass.bass_isa.ReduceOp.max).then_inc(dmax_ready, 1)
                split(L)
                pool.wait_ge(whmean_ready, L + 1)
                with pool.Fori(0, GROUPS) as g:
                    finish(L, g)

        @block.vector
        def _(dve):
            dve.sem_inc(conv, 4)
            dve.sem_inc(wh_free, 2)
            dve.sem_inc(parts_ready[0], 2)
            links = [0]

            def link(ins):
                links[0] += 1
                ins.then_inc(chain, 1)
                dve.wait_ge(chain, links[0])

            def constants():
                nc.vector.memset(ones[:, :], 1.0)
                nc.vector.memset(waug[:, :, :, :], 0.0)
                nc.vector.memset(zero_w[:, :], 0.0).then_inc(const_dve, 1)
                by_bit = power.rearrange("p (b w e) -> p b w e", b=8, w=WPT)
                for b in range(8):
                    for e in range(2):
                        ins = nc.vector.memset(by_bit[:, b, :, e], float(2 ** (b + 8 * e)))
                link(ins)
                dve.wait_ge(const_pool, 2)
                link(nc.vector.tensor_tensor(hot, ident[:, :], power, ALU.mult))
                link(nc.vector.tensor_reduce(packing_sum, hot.rearrange("p (b w e) -> p w b e", b=8, w=WPT), AX.XY,
                                             ALU.add))
                nc.vector.tensor_copy(pack_w[:, :], packing_sum).then_inc(const_dve, 1)
                dve.wait_ge(const_pe, 1)
                nc.vector.tensor_copy(wcol[:, :, :], psum[0:F, 0, 0:2 * F].rearrange("p (l f) -> p l f", l=2)
                                      ).then_inc(const_dve, 1)
                dve.wait_ge(const_pe, 2)
                nc.vector.tensor_copy(waug[0:F, :, 0, F:F + 2], psum[0:F, 1, 0:4].rearrange("p (l k) -> p l k", l=2))
                nc.vector.tensor_copy(waug[0:F, 0, 0, 0:F], wrow[:, 0, :])
                nc.vector.tensor_copy(waug[0:F, 1, 0, 0:F], wcol[:, 1, :]).then_inc(const_dve, 1)

            def convert(eights, s):
                dve.wait_ge(stage_in[s % 4], (eights * 2 + (s // 4 + 1)) * 16)
                dve.wait_ge(packed, eights * 8 + (s + 1))
                nc.vector.tensor_scalar(natural[:, s % NAT, :], stage[:, s % 4, :], 0, float(ONE8),
                                        ALU.is_gt, ALU.mult).then_inc(conv, 1)

            def normalise(L, span):
                q0, q1 = SPANS[L][span]

                def spread_of(q):
                    t = slice(q * QT, (q + 1) * QT)
                    dve.wait_ge(squared, 4 * L + q + 1)
                    nc.vector.tensor_reduce(var[:, t], square[L][q], AX.X, ALU.add).then_inc(var_sums, 1)
                    if L == 1:
                        dve.sem_inc(squares_used, 1)

                for q in range(q0, q1):
                    t = slice(q * QT, (q + 1) * QT)
                    dve.wait_ge(x_in[q], 16 * (L + 1))
                    link(nc.vector.tensor_reduce(mean[:, t], xall[L][:, t, :], AX.X, ALU.add))
                    link(nc.vector.tensor_scalar(mean[:, t], mean[:, t], -1.0 / F, None, ALU.mult))
                    nc.vector.tensor_tensor(xall[L][:, t, :], xall[L][:, t, :],
                                            mean[:, t].unsqueeze(2).to_broadcast((P, QT, F)),
                                            ALU.add).then_inc(centred, 1)
                    if q > q0:
                        spread_of(q - 1)
                spread_of(q1 - 1)
                dve.wait_ge(var_sums, 4 * L + q1)
                t = slice(q0 * QT, q1 * QT)
                nc.vector.tensor_scalar(var[:, t], var[:, t], 1.0 / F, EPS, ALU.mult, ALU.add).then_inc(var_ready, 1)
                if L == 0:
                    for s in range(4):
                        convert(0, s)

            def invert_std(L, span):
                q0, q1 = SPANS[L][span]
                t = slice(q0 * QT, q1 * QT)
                dve.wait_ge(std_ready, L + span + 1)
                link(nc.vector.reciprocal(rstd[:, t], std[:, t]))
                link(nc.vector.tensor_tensor(newton[:, t], rstd[:, t], rstd[:, t], ALU.mult))
                link(nc.vector.tensor_tensor(newton[:, t], newton[:, t], var[:, t], ALU.mult))
                link(nc.vector.tensor_scalar(newton[:, t], newton[:, t], -0.5, 1.5, ALU.mult, ALU.add))
                link(nc.vector.tensor_tensor(rstd[:, t], rstd[:, t], newton[:, t], ALU.mult))

            def take_wh(L, i):
                for k in range(QB):
                    b = i * QB + k
                    if L == 0:
                        convert(i, 4 + 2 * k)
                        convert(i, 5 + 2 * k)
                    dve.wait_ge(wh_mm, b + (L * GROUPS + 1))
                    got = psum[:, PROJ[L] + k % 2, 0:GT * (F + 2)].rearrange("p (t f) -> p t f", t=GT)
                    t = bass.ds(b * GT, GT)
                    nc.vector.tensor_tensor(wh[:, t, :], got[:, :, 0:F],
                                            rstd[:, t].unsqueeze(2).to_broadcast((P, GT, F)), ALU.mult)
                    nc.vector.tensor_tensor(sd[:, t, :], got[:, :, F:F + 2],
                                            rstd[:, t].unsqueeze(2).to_broadcast((P, GT, 2)),
                                            ALU.mult).then_inc(wh_free, 1)
                    dve.wait_ge(wh_free, b + (L * GROUPS + 3))
                    ins = nc.vector.tensor_reduce(block_top[:, bass.ds(b, 1)], wh[:, t, :], AX.XY, ALU.max,
                                                  apply_absolute_value=True)
                ins.then_inc(tops_found, 1)

            def prepare(L):
                dve.wait_ge(wh_free, 2 + (L + 1) * GROUPS)
                dve.wait_ge(tops_found, (L + 1) * 4)
                link(nc.vector.tensor_scalar(minus_d[:, :], sd[:, :, 1], -1.0, None, ALU.mult))
                nc.vector.tensor_reduce(tops[:, 0:1], sd[:, :, 1], AX.X, ALU.max)
                nc.vector.tensor_reduce(tops[:, 2:3], minus_d[:, :], AX.X, ALU.max)
                nc.vector.tensor_reduce(tops[:, 1:2], block_top[:, :], AX.X, ALU.max).then_inc(dmax_part, 1)
                if L == 0:
                    for s in range(GSTEPS + 4, GSTEPS + AHEAD - 2):
                        convert(s // 8, s % 8)
                nc.vector.tensor_scalar(steep_d[:, :], sd[:, :, 1], STEEP, None, ALU.mult)
                dve.wait_ge(dmax_ready, L + 1)
                nc.vector.tensor_scalar(shift[:, 0:1], top[:, 0:1], -1.0, None, ALU.mult)
                nc.vector.tensor_scalar(shift[:, 1:2], top[:, 0:1], -LEAK, None, ALU.mult)
                link(nc.vector.tensor_scalar(shift[:, 3:4], top[:, 1:2], 1.0, 1.0 / TOP, ALU.max, ALU.mult))
                nc.vector.reciprocal(shift[:, 2:3], shift[:, 3:4])
                link(nc.vector.tensor_tensor(beyond[:, 0:1], top[:, 0:1], top[:, 2:3], ALU.add))
                nc.vector.tensor_scalar(beyond[:, 0:1], beyond[:, 0:1], SPREAD, None, ALU.is_gt)
                link(nc.vector.tensor_scalar(beyond[:, 1:2], top[:, 1:2], TALL, None, ALU.is_gt))
                nc.vector.tensor_tensor(unsafe[:, L:L + 1], beyond[:, 0:1], beyond[:, 1:2], ALU.add
                                        ).then_inc(unsafe_ready, 1)
                link(nc.vector.tensor_scalar(zc[:, 0, :], sd[:, :, 0], top[:, 0:1], None, ALU.add))
                link(nc.vector.tensor_scalar(zc[:, 1, :], zc[:, 0, :], LEAK, None, ALU.mult))
                link(nc.vector.tensor_tensor(newton[:, :], zc[:, 0, :], zc[:, 1, :], ALU.max))
                nc.vector.tensor_tensor(zc[:, 2, :], zc[:, 0, :], newton[:, :], ALU.subtract)
                nc.vector.tensor_tensor(zc[:, 3, :], zc[:, 1, :], newton[:, :], ALU.subtract).then_inc(exp_in, 1)
                dve.wait_ge(exp_ready, L + 1)
                nc.vector.tensor_scalar(uv[:, :, :], uv[:, :, :], shift[:, 3:4], None, ALU.mult)
                link(nc.vector.tensor_scalar(dg[:, :, :], dg[:, :, :], shift[:, 2:3], None, ALU.mult))
                dve.sem_inc(factors, 1)
                for e in range(2):
                    ins = nc.vector.tensor_copy(parts[e][:, :, 0, F], dg[:, e, :])
                link(ins)
                for e in range(2):
                    nc.vector.tensor_tensor(parts[e][:, :, 1, F], dg[:, e, :], parts[e][:, :, 0, F], ALU.subtract)
                with dve.Fori(0, SPLITS // 2) as i:
                    dve.wait_ge(parts_ready[0], i * 2 + (L * SPLITS + 2))
                    for k in range(2):
                        t = bass.ds((i * 2 + k) * SB, SB)
                        nc.vector.tensor_tensor(rest[:, 0, k, :, :], wh[:, t, :],
                                                dg[:, 0, t].unsqueeze(2).to_broadcast((P, SB, F)),
                                                ALU.mult).then_inc(scaled[0], 1)
                    for k in range(2):
                        t = bass.ds((i * 2 + k) * SB, SB)
                        dve.wait_ge(hi_ready[0], i * 2 + (L * SPLITS + k + 1))
                        nc.vector.tensor_tensor(parts[0][:, t, 1, 0:F], rest[:, 0, k, :, :], parts[0][:, t, 0, 0:F],
                                                ALU.subtract).then_inc(parts_ready[0], 1)
                if L == 0:
                    for s in range(GSTEPS + AHEAD - 2, GSTEPS + AHEAD):
                        convert(s // 8, s % 8)
                dve.wait_ge(whmean_mm, L + 1)
                link(nc.vector.tensor_reduce(whsum[:, :], psum[:, PROJ[L] + 1, 0:8 * F].rearrange("p (t f) -> p f t", t=8),
                                             AX.X, ALU.add))
                nc.vector.tensor_scalar(whmean[:, :], whsum[:, :], 1.0 / N, None, ALU.mult).then_inc(whmean_ready, 1)
                dve.wait_ge(parts_ready[1], (L + 1) * SPLITS + 2)
                dve.wait_ge(parts_ready[0], (L + 1) * SPLITS + 2)

            GEN_STEPS = 5 * LC + 6 + 3 * LC + 3 + 7

            def general(L):
                dve.sem_inc(gen_masked[L], 1)
                with dve.Fori(0, TILES) as r:
                    done = [0]

                    def link(ins):
                        done[0] += 1
                        ins.then_inc(gen_step[L], 1)
                        dve.wait_ge(gen_step[L], r * GEN_STEPS + done[0])

                    for c in range(LC):
                        dve.wait_ge(gen_in[L], r * (LC * 32) + (c + 1) * 32)
                        link(nc.vector.tensor_scalar(scores[c], adj_chunk, 0, None, ALU.is_gt))
                        link(nc.vector.tensor_tensor(masked_d, scores[c], d_row, ALU.mult))
                        link(nc.vector.tensor_scalar(scores[c], scores[c], FAR, -FAR, ALU.mult, ALU.add))
                        link(nc.vector.tensor_tensor(scores[c], scores[c], masked_d, ALU.add))
                        dve.sem_inc(gen_masked[L], 1)
                        link(nc.vector.tensor_reduce(chunk_max[:, c:c + 1], scores[c], AX.X, ALU.max))
                    link(nc.vector.tensor_copy(s_cur, sd[:, bass.ds(r, 1), 0]))
                    link(nc.vector.tensor_reduce(row_max, chunk_max, AX.X, ALU.max))
                    link(nc.vector.tensor_tensor(row_max, row_max, s_cur, ALU.add))
                    link(nc.vector.tensor_scalar(row_leak, row_max, LEAK, None, ALU.mult))
                    link(nc.vector.tensor_tensor(row_max, row_max, row_leak, ALU.max))
                    link(nc.vector.tensor_scalar(minus_max, row_max, -1.0, None, ALU.mult))
                    for c in range(LC):
                        link(nc.vector.tensor_scalar(scores[c], scores[c], s_cur, None, ALU.add))
                        link(nc.vector.tensor_scalar(leaked, scores[c], LEAK, None, ALU.mult))
                        link(nc.vector.tensor_tensor(scores[c], scores[c], leaked, ALU.max))
                        dve.sem_inc(gen_scores[L], 1)
                    for c in range(LC):
                        dve.wait_ge(gen_probs[L], r * LC + (c + 1))
                        ins = nc.vector.tensor_reduce(chunk_sum[:, c:c + 1], scores[c], AX.X, ALU.add)
                    link(ins)
                    link(nc.vector.tensor_reduce(row_sum, chunk_sum, AX.X, ALU.add))
                    link(nc.vector.reciprocal(row_inv, row_sum))
                    dve.wait_ge(gen_mm[L], (r + 1) * LC + 1)
                    link(nc.vector.tensor_scalar(y_gen, psum[:, 2, 0:F], row_inv, None, ALU.mult))
                    nc.vector.tensor_scalar(hneg[:, 0, :], y_gen, 0.0, None, ALU.min).then_inc(gen_neg[L], 1)
                    dve.wait_ge(gen_tanh[L], r + 1)
                    link(nc.vector.tensor_scalar(hneg[:, 0, :], th[:, 0, :], -0.5, 0.5, ALU.mult, ALU.add))
                    link(nc.vector.reciprocal(hneg[:, 0, :], hneg[:, 0, :]))
                    link(nc.vector.tensor_tensor(hneg[:, 0, :], hneg[:, 0, :], th[:, 0, :], ALU.mult))
                    link(nc.vector.tensor_scalar(y_gen, y_gen, 0.0, None, ALU.max))
                    link(nc.vector.tensor_tensor(y_gen, y_gen, hneg[:, 0, :], ALU.add))
                    dve.wait_ge(gen_x_in[L], (r + 1) * 16)
                    link(nc.vector.tensor_tensor(y_gen, y_gen, x_gen, ALU.add))
                    dve.sem_inc(gen_y[L], 1)
                    assert done[0] == GEN_STEPS, done[0]

            def unpack(L, g, u):
                n = (g + L * GROUPS) * CHUNKS + (u - UNPACKED + 1) * CPU
                if not (isinstance(g, int) and n <= 0):
                    dve.wait_ge(chunk_used, n + TOG)
                w = words[:, u * UT:(u + 1) * UT, bass.ds(g * (GT * WPT), GT * WPT)].rearrange(
                    "p t (k m) -> p t k m", k=GT)
                b_out = work[:, (u % UNPACKED) * UT * GROUP:(u % UNPACKED + 1) * UT * GROUP].bitcast(U16).rearrange(
                    "p (t k b m) -> p t k b m", t=UT, k=GT, b=8)
                for b in range(8):
                    up = 6 - b
                    ins = nc.vector.tensor_scalar(
                        b_out[:, :, :, b, :], w, abs(up), MARKS,
                        ALU.logical_shift_left if up >= 0 else ALU.logical_shift_right, ALU.bitwise_and)
                ins.then_inc(unpacked, 1)

            def own_signs(L, g, c):
                gg = g + L * GROUPS
                dve.wait_ge(chunk_used, gg * CHUNKS + c + 1)
                dve.wait_ge(row_in, (gg + 1) * 16)
                row = (s_row[:, g % 2, :] if isinstance(g, int)
                       else s_row[:, bass.ds(g % 2, 1), :].rearrange("p o i -> p (o i)"))
                for j in range(CT - DVE_SIGNS, CT):
                    t = c * CT + j
                    ins = nc.vector.tensor_scalar(tog[:, c % TOG, j, :], row, minus_d[:, t:t + 1], float(MARK),
                                                  ALU.is_gt, ALU.mult)
                ins.then_inc(signs_dve, 1)

            def masks(L, g, c, between):
                n = (g + L * GROUPS) * CHUNKS + c
                edge = bits[:, (c // CPU) % UNPACKED, (c % CPU) * CT:(c % CPU + 1) * CT, :].rearrange(
                    "p j i -> p (j i)").bitcast(I32)
                pos = tog[:, c % TOG, :, :].rearrange("p j i -> p (j i)").bitcast(I32)
                if shared(L, g):
                    if c == 0:
                        own_signs(L, g, 0)
                    dve.wait_ge(signs_dve, n - UNSHARED + 1)
                between(0)
                dve.wait_ge(sign_ready, n + 1)
                if c % CPU == 0:
                    dve.wait_ge(unpacked, (g + L * GROUPS) * UNPACKS + c // CPU + 1)
                nc.vector.tensor_tensor(pos, edge, pos, ALU.bitwise_and).then_inc(anded, 1)
                between(1)
                if shared(L, g) and c + 1 < CHUNKS:
                    own_signs(L, g, c + 1)
                dve.wait_ge(anded, n + 1)
                nc.vector.tensor_tensor(edge, edge, pos, ALU.bitwise_xor).then_inc(masks_ready, 1)
                between(2)

            def invert_den(L, g):
                dve.wait_ge(den_ready, g + (L * GROUPS + 1))
                nc.vector.reciprocal(rden[:, :, :], den[:, :, :]).then_inc(den_inv, 1)

            def group(L, g, limit, first):
                if L == 0:
                    dve.wait_ge(stored, g * GT + (GT + 2))
                for c in range(CHUNKS):
                    if c % CPU == 0:
                        unpack(L, g, c // CPU)

                    def between(k):
                        for s in steps_at(c, limit)[(0, 1, 2)[k]:(1, 2, PACE)[k]]:
                            convert((g + 1) * (GSTEPS // 8), s)
                    masks(L, g, c, between)
                    if not first:
                        if c == 2:
                            invert_den(L, g - 1)

            constants()
            normalise(0, 0)
            invert_std(0, 0)
            with dve.Fori(0, 4) as i:
                take_wh(0, i)
            prepare(0)
            when_unsafe(dve, 0, lambda: general(0))
            group(0, 0, ALL, True)
            with dve.Fori(1, GROUPS - 2) as g:
                group(0, g, ALL, False)
            group(0, GROUPS - 2, GSTEPS, False)
            group(0, GROUPS - 1, 0, False)
            normalise(1, 0)
            invert_den(0, GROUPS - 1)
            invert_std(1, 0)
            with dve.Fori(0, EARLY) as i:
                take_wh(1, i)
            normalise(1, 1)
            invert_std(1, 1)
            take_wh(1, EARLY)
            prepare(1)
            when_unsafe(dve, 1, lambda: general(1))
            group(1, 0, 0, True)
            with dve.Fori(1, GROUPS) as g:
                group(1, g, 0, False)
            invert_den(1, GROUPS - 1)

        @block.tensor
        def _(pe):
            pe.sem_inc(packed, NAT)
            pe.sem_inc(chunk_used, TOG)

            def constants():
                pe.wait_ge(const_in, 96)
                pe.wait_ge(const_pool, 2)
                for l in range(2):
                    ins = nc.tensor.transpose(psum[0:F, 0, l * F:(l + 1) * F], wrow[:, l, :], ident[0:F, 0:F])
                ins.then_inc(const_pe, 1)
                pe.wait_ge(const_dve, 3)
                nc.tensor.matmul(psum[0:F, 1, 0:2], wcol[:, 0, :], acol[:, 0, :], start=True, stop=True)
                nc.tensor.matmul(psum[0:F, 1, 2:4], wrow[:, 1, :], acol[:, 1, :], start=True, stop=True
                                 ).then_inc(const_pe, 1)
                pe.wait_ge(const_dve, 4)
                pe.wait_ge(waug_twice, 16)

            def pack(g, s):
                step = g * GSTEPS + s
                k = s // STEPS
                pe.wait_ge(conv, step + 5)
                if s % STEPS == 0:
                    pe.wait_ge(stored, g * GT + k + 1)
                settled(pe)
                for j in range(LT):
                    t = (s % STEPS) * LT + j
                    ins = nc.tensor.matmul(psum[:, 4 + k % 2, t * WPT:(t + 1) * WPT],
                                           natural[:, s % NAT, j * P:(j + 1) * P].bitcast(FP8), pack_w[:, :],
                                           start=True, stop=True)
                ins.then_inc(packed, 1)

            def prepare(L):
                def turn(b):
                    if b % QB == 0:
                        pe.wait_ge(centred, 4 * L + b // QB + 1)
                    for j in range(GT // 2):
                        t = b * GT + 2 * j
                        ins = nc.tensor.transpose(psum[:, TURN[L] + b % 2, j * P:(j + 1) * P],
                                                  xall[L][:, t:t + 2, :].rearrange("p t f -> p (t f)"), ident[:, :])
                    ins.then_inc(turned, 1)

                def project(b):
                    pe.wait_ge(ht_ready, L * GROUPS + b + 1)
                    pe.wait_ge(wh_free, L * GROUPS + b + 1)
                    for j in range(GT // 2):
                        ins = nc.tensor.matmul(psum[:, PROJ[L] + b % 2, j * 2 * (F + 2):(j + 1) * 2 * (F + 2)],
                                               ht[:, b % 2, j * P:(j + 1) * P],
                                               waug[:, L, :, :].rearrange("p k f -> p (k f)"),
                                               start=True, stop=True)
                    ins.then_inc(wh_mm, 1)

                turn(0)
                turn(1)
                if L == 0:
                    for s in range(4):
                        pack(0, s)
                for b in range(GROUPS):
                    late = L == 1 and b + 1 == EARLY * QB
                    if 0 < b < GROUPS - 1 and not late:
                        turn(b + 1)
                    project(b)
                    if late:
                        turn(b + 1)
                    if L == 0 and b > 0:
                        pack(0, 2 * b + 2)
                        pack(0, 2 * b + 3)
                if L == 0:
                    for s in range(GSTEPS + 2, GSTEPS + 4):
                        pack(0, s)
                pe.wait_ge(wh_free, 2 + (L + 1) * GROUPS)
                nc.tensor.transpose(psum[0:TILES, TURN[L], 0:P], sd[:, :, 0], ident[:, :]).then_inc(s_turn, 1)
                for k in range(TILES // 8):
                    ins = nc.tensor.matmul(psum[:, PROJ[L] + 1, 0:8 * F], ones[:, :],
                                           wh[:, k * 8:(k + 1) * 8, :].rearrange("p t f -> p (t f)"),
                                           start=k == 0, stop=k == TILES // 8 - 1)
                ins.then_inc(whmean_mm, 1)
                if L == 0:
                    for s in range(GSTEPS + 4, GSTEPS + AHEAD):
                        pack(0, s)

            def general(L):
                nc.tensor.transpose(psum[0:TILES, TURN[L] + 1, 0:P], sd[:, :, 1], ident[:, :]).then_inc(gen_d_turn[L], 1)
                pe.sem_inc(gen_mm[L], 1)
                with pe.Fori(0, TILES) as r:
                    for c in range(LC):
                        pe.wait_ge(gen_probs[L], r * LC + (c + 1))
                        settled(pe)
                        for k in range(LT):
                            ins = nc.tensor.transpose(psum[:, k // 4, (k % 4) * P:(k % 4 + 1) * P],
                                                      scores[c][:, k * P:(k + 1) * P], ident[:, :])
                        ins.then_inc(gen_turned[L], 1)
                        pe.wait_ge(gen_lhs[L], r * LC + (c + 1))
                        settled(pe)
                        for k in range(LT):
                            t = c * LT + k
                            ins = nc.tensor.matmul(psum[:, 2, 0:F], probs_t[:, k, :], wh[:, t, :],
                                                   start=t == 0, stop=t == TILES - 1)
                        ins.then_inc(gen_mm[L], 1)

            def group(L, g, limit):
                gg = g + L * GROUPS
                for c in range(CHUNKS):
                    n = gg * CHUNKS + c
                    for s in steps_at(c, limit)[:2]:
                        pack(g + 1, s)
                    pe.wait_ge(masks_ready, n + 1)
                    settled(pe)
                    for r in range(GT):
                        if c == 0:
                            pe.wait_ge(bank_free, gg * GT + r + 1)
                            nc.tensor.matmul(psum[:, r, 0:COLS[2]], zero_w[:, 0:P], zero_w[:, 0:COLS[2]],
                                             start=True, stop=False, skip_group_check=True)
                        for j in range(CT):
                            t = c * CT + j
                            for e, mask in ((0, tog[:, c % TOG, j, r * P:(r + 1) * P]),
                                            (1, bits[:, (c // CPU) % UNPACKED, (c % CPU) * CT + j, r * P:(r + 1) * P])):
                                ins = nc.tensor.matmul(psum[:, r, COLS[e]:COLS[e + 1]], mask.bitcast(FP8),
                                                       parts[e][:, t, :, :].rearrange("p k h -> p (k h)"),
                                                       start=False, stop=(c == CHUNKS - 1 and j == CT - 1),
                                                       skip_group_check=True)
                        if c == CHUNKS - 1 and r < GT - 1:
                            ins.then_inc(bank_done, 1)
                    if c == CHUNKS - 1:
                        ins.then_inc(chunk_used, 1)
                        pe.wait_ge(chunk_used, n + 1 + TOG)
                        pe.sem_inc(bank_done, 1)
                    else:
                        ins.then_inc(chunk_used, 1)
                    for s in steps_at(c, limit)[2:]:
                        pack(g + 1, s)

            constants()
            prepare(0)
            when_unsafe(pe, 0, lambda: general(0))
            for L in range(2):
                if L == 1:
                    prepare(1)
                    when_unsafe(pe, 1, lambda: general(1))
                for e in range(2):
                    pe.wait_ge(parts_ready[e], (L + 1) * SPLITS + 2)
                if L == 0:
                    with pe.Fori(0, GROUPS - 2) as g:
                        group(0, g, ALL)
                    group(0, GROUPS - 2, GSTEPS)
                    group(0, GROUPS - 1, 0)
                else:
                    with pe.Fori(0, GROUPS) as g:
                        group(1, g, 0)


_INS = ["x", "adj", "L0_gnn_W", "L0_gnn_a", "L1_gnn_W", "L1_gnn_a"]


def kernel(**inputs):
    import concourse.bacc as _bacc
    from concourse import mybir as _mybir
    from concourse.bass_utils import run_bass_kernel_spmd as _run

    nc = _bacc.Bacc("TRN2", target_bir_lowering=False, num_devices=1)
    arrays, args = {}, []
    for name in _INS:
        a = np.ascontiguousarray(inputs[name])
        arrays[f"in_{name}_dram"] = a
        args.append(nc.dram_tensor(f"in_{name}_dram", a.shape, _mybir.dt.from_np(a.dtype), kind="ExternalInput").ap())
    args.append(nc.dram_tensor("out_dram", inputs["x"].shape, _mybir.dt.float32, kind="ExternalOutput").ap())
    gat2_kernel(nc, *args)
    r = _run(nc, [arrays], core_ids=[0])
    return r.results[0]["out_dram"]
```
